# Optimizing a Trainium2 kernel written in Bass

```python
import numpy as np
import jax
import jax.numpy as jnp

def _softmax(x, axis=-1):
    return jax.nn.softmax(x, axis=axis)

def _gelu(x):
    return jax.nn.gelu(x, approximate=True)

def _silu(x):
    return jax.nn.silu(x)

def _sigmoid(x):
    return jax.nn.sigmoid(x)

def _layernorm(x, axis=-1, eps=1e-05):
    m = jnp.mean(x, axis=axis, keepdims=True)
    v = jnp.var(x, axis=axis, keepdims=True)
    return (x - m) / jnp.sqrt(v + eps)

def _scatter_add(tgt, idx, src, axis=0):
    return tgt.at[idx].add(src)

def _segment_sum(src, seg, n):
    return jax.ops.segment_sum(src, seg, n)
kernel_name = 'mk_gnn_preln_d1_gnn_r8_4d08a3'

def setup_inputs(seed: int=0):
    np.random.seed(seed)
    _w = jnp.asarray

    def _rec_inputs():
        import jax
        import jax.numpy as jnp
        _gk = jax.random.key(seed)
        x = -0.000202 + 1 * jax.random.normal(jax.random.fold_in(_gk, 1), (12500, 64), jnp.float32)
        src = jax.random.randint(jax.random.fold_in(_gk, 2), (400000,), 0, 12500, jnp.int32)
        dst = jax.random.randint(jax.random.fold_in(_gk, 3), (400000,), 0, 12500, jnp.int32)
        _o = jnp.argsort(dst, stable=True)
        src = src[_o]
        dst = dst[_o]
        edge_attr_32 = -5.16925e-05 + 1.00005 * jax.random.normal(jax.random.fold_in(_gk, 12), (400000, 32), jnp.float32)
        return (x, src, dst, edge_attr_32)
    x, src, dst, edge_attr_32 = _rec_inputs()

    def _L0_gnn_setup():
        import jax, jax.numpy as jnp
        import numpy as np
        N_NODES = 12500
        N_EDGES = 400000
        EDGE_OUT = 32
        HID = 128
        NODE_OUT = 64
        N_GRAPHS = 16
        key = jax.random.key(seed)
        ks = jax.random.split(key, 9)
        x = jax.random.normal(ks[0], (N_NODES, 64), dtype=jnp.float32)
        edge_index = jax.random.randint(ks[1], (2, N_EDGES), 0, N_NODES, dtype=jnp.int64)
        edge_attr = jax.random.normal(ks[2], (N_EDGES, EDGE_OUT), dtype=jnp.float32)
        u = jax.random.normal(ks[3], (N_GRAPHS, 1), dtype=jnp.float32)
        batch = jnp.sort(jax.random.randint(ks[4], (N_NODES,), 0, N_GRAPHS, dtype=jnp.int64))
        d_in = 3 * EDGE_OUT + 1
        W1 = jax.random.normal(ks[5], (d_in, HID), dtype=jnp.float32) / np.sqrt(d_in)
        b1 = jnp.zeros((HID,), dtype=jnp.float32)
        W2 = jax.random.normal(ks[6], (HID, NODE_OUT), dtype=jnp.float32) / np.sqrt(HID)
        b2 = jnp.zeros((NODE_OUT,), dtype=jnp.float32)
        return {'x': x, 'edge_index': edge_index, 'edge_attr': edge_attr, 'u': u, 'batch': batch, 'W1': W1, 'b1': b1, 'W2': W2, 'b2': b2}
    _L0_gnn_all = _L0_gnn_setup()
    _L0_gnn_in = {k: v for k, v in _L0_gnn_all.items() if k in ('u', 'W1', 'b1', 'W2', 'b2')}
    del _L0_gnn_all
    return {'x': x, 'src': src, 'dst': dst, 'edge_attr_32': edge_attr_32, 'L0_gnn_u': _L0_gnn_in['u'], 'L0_gnn_W1': _L0_gnn_in['W1'], 'L0_gnn_b1': _L0_gnn_in['b1'], 'L0_gnn_W2': _L0_gnn_in['W2'], 'L0_gnn_b2': _L0_gnn_in['b2']}

def reference(x, src, dst, edge_attr_32, L0_gnn_u, L0_gnn_W1, L0_gnn_b1, L0_gnn_W2, L0_gnn_b2):
    import jax
    import jax.numpy as jnp

    def _L0_gnn_ref(x, edge_index, edge_attr, u, batch, W1, b1, W2, b2):
        import jax, jax.numpy as jnp
        import numpy as np
        N_NODES = 12500
        N_EDGES = 400000
        EDGE_OUT = 32
        HID = 128
        NODE_OUT = 64
        N_GRAPHS = 16
        N = x.shape[0]
        row = edge_index[0]
        seg_sum = jax.ops.segment_sum(edge_attr, row, num_segments=N)
        seg_max = jax.ops.segment_max(edge_attr, row, num_segments=N)
        cnt = jax.ops.segment_sum(jnp.ones((edge_attr.shape[0], 1), edge_attr.dtype), row, num_segments=N)
        seg_mean = seg_sum / jnp.maximum(cnt, 1.0)
        seg_max = jnp.where(cnt > 0, seg_max, 0.0)
        h = jnp.concatenate([seg_sum, seg_max, seg_mean, u[batch]], axis=1)
        h = jax.nn.relu(h @ W1 + b1)
        return h @ W2 + b2
    edge_index = jnp.stack([src, dst])
    batch0 = jnp.zeros((12500,), jnp.int32)
    h = jnp.maximum(_layernorm(x, axis=-1), 0.0)
    x = x + _L0_gnn_ref(h, edge_index, edge_attr_32, L0_gnn_u, batch0, L0_gnn_W1, L0_gnn_b1, L0_gnn_W2, L0_gnn_b2)
    return x

_drawn_inputs = setup_inputs


def setup_inputs(seed=0):
    import zlib

    import numpy as np

    out = dict(_drawn_inputs(seed))
    spreads = {'L0_gnn_b1': (0.0, 0.289), 'L0_gnn_b2': (0.0, 0.1)}
    factors = {'L0_gnn_u': 3.002}
    for name, (base, spread) in spreads.items():
        noise = np.random.default_rng([zlib.crc32(name.encode()), seed]).standard_normal(out[name].shape)
        drawn = base * np.exp(spread * noise) if base else spread * noise
        out[name] = jnp.asarray(drawn.astype(out[name].dtype))
    for name, factor in factors.items():
        out[name] = (out[name] * factor).astype(out[name].dtype)
    return out
```

```python
from contextlib import ExitStack

import numpy as np

import concourse.bass as bass
from concourse import mybir

FP32 = mybir.dt.float32
BF16 = mybir.dt.bfloat16
I32 = mybir.dt.int32
ALU = mybir.AluOpType
ACT = mybir.ActivationFunctionType
AXIS_X = mybir.AxisListType.X
FLT_MAX = float(np.finfo(np.float32).max)


def build(nc, x, src, edge_attr, u, w1, b1, w2, b2, out, rows):
    P = 128
    EDGES, FEAT = edge_attr.shape
    NODES, NODE_OUT = x.shape
    HID = w1.shape[1]
    BLOCKS = -(-NODES // P)
    TILES = EDGES // P
    GROUP = 5
    GROUPS = 5
    CHUNK = GROUP * GROUPS
    CHUNKS = TILES // CHUNK
    assert EDGES == P * CHUNK * CHUNKS
    WINDOW = 64
    SLOTS = 7
    ROUNDS = BLOCKS // SLOTS
    assert ROUNDS * SLOTS == BLOCKS
    CAT = 3 * FEAT
    FULL_P = NODES // BLOCKS
    REST = NODES - FULL_P * BLOCKS
    BANK_COLS = 512

    src_view = src.rearrange("(p t) -> p t", p=P)
    edge_view = edge_attr.rearrange("(p t) f -> p (t f)", p=P)

    ctx = ExitStack()
    with ctx:
        def sb(name, shape, dt):
            return ctx.enter_context(nc.sbuf_tensor(name, shape, dt))

        def ps(name, shape, dt):
            return ctx.enter_context(nc.psum_tensor(name, shape, dt))

        def sem(name):
            return ctx.enter_context(nc.semaphore(name))

        iota_i = sb("iota_i", [P, P], I32)
        iota_b = sb("iota_b", [P, P], BF16)
        iota_f = sb("iota_f", [P, WINDOW], FP32)
        before_f = sb("before_f", [P, P], FP32)
        before_b = sb("before_b", [P, P], BF16)
        ident_f = sb("ident_f", [P, P], FP32)
        ident_b = sb("ident_b", [P, P], BF16)
        zeros_b = sb("zeros_b", [P, P], BF16)
        zeros_f = sb("zeros_f", [P, P], FP32)
        src_i = sb("src_i", [P, TILES], I32)
        run_sum = sb("run_sum", [P, BLOCKS, FEAT], FP32)
        run_max = sb("run_max", [P, BLOCKS, FEAT], FP32)
        owner = run_sum[:, :, :].rearrange("p b f -> p (b f)")[:, 0:TILES]
        block_of = run_max[:, :, :].rearrange("p b f -> p (b f)")[:, 0:TILES]
        owner_c = sb("owner_c", [P, CHUNK], FP32)
        block_c = sb("block_c", [P, CHUNK], FP32)
        hot_block = sb("hot_block", [P, CHUNK, BLOCKS], BF16)
        hot_owner = sb("hot_owner", [P, CHUNK, P], BF16)
        hot_block_t = sb("hot_block_t", [BLOCKS, GROUPS, GROUP * P], BF16)
        hot_block_tf = sb("hot_block_tf", [BLOCKS, GROUPS, GROUP * P], FP32)
        earlier = sb("earlier", [P, GROUPS, GROUP * P], BF16)
        start_sb = sb("start_sb", [BLOCKS, GROUP, P], FP32)
        picked = sb("picked", [P, GROUP, P], BF16)
        position_f = sb("position_f", [P, CHUNK], FP32)
        position = sb("position", [P, CHUNK], I32)
        edges = sb("edges", [P, GROUPS, GROUP * FEAT], FP32)
        count = sb("count", [BLOCKS, P], FP32)
        cumul = sb("cumul", [BLOCKS, P], FP32)
        block_base = sb("block_base", [BLOCKS, 1], FP32)
        offset = sb("offset", [BLOCKS, P], FP32)
        count_t = sb("count_t", [P, BLOCKS], FP32)
        left_t = sb("left_t", [P, BLOCKS], FP32)
        next_t = sb("next_t", [P, BLOCKS], FP32)
        most_p = sb("most_p", [P, 1], FP32)
        most = sb("most", [1, 1], FP32)
        passes_i = sb("passes_i", [1, 1], I32)
        window = sb("window", [P, SLOTS, WINDOW * FEAT], FP32)
        clipped = sb("clipped", [P, WINDOW * FEAT], FP32)
        window_at = sb("window_at", [P, SLOTS], I32)
        left_s = sb("left_s", [P, SLOTS], FP32)
        half = sb("half", [P, WINDOW], FP32)
        bound = sb("bound", [P, WINDOW], FP32)
        keep = sb("keep", [P, WINDOW], I32)
        part_sum = sb("part_sum", [P, SLOTS, FEAT], FP32)
        part_max = sb("part_max", [P, SLOTS, FEAT], FP32)
        divisor = sb("divisor", [P, BLOCKS], FP32)
        nonempty = sb("nonempty", [P, BLOCKS], FP32)
        w1_sb = sb("w1_sb", [CAT, HID], FP32)
        w1_u = sb("w1_u", [HID, 1], FP32)
        b1_sb = sb("b1_sb", [HID, 1], FP32)
        u_sb = sb("u_sb", [HID, 1], FP32)
        bias1 = sb("bias1", [HID, 1], FP32)
        w2_sb = sb("w2_sb", [HID, NODE_OUT], FP32)
        b2_sb = sb("b2_sb", [P, NODE_OUT], FP32)
        x_sb = sb("x_sb", [P, BLOCKS * NODE_OUT], FP32)
        cat = sb("cat", [P, SLOTS, CAT], FP32)
        cat_t = sb("cat_t", [CAT, SLOTS * P], FP32)
        hidden = sb("hidden", [HID, SLOTS * P], FP32)

        start_ps = ps("start_ps", [P, BANK_COLS], FP32)
        hot_t_ps = ps("hot_t_ps", [P, 2 * BANK_COLS], BF16)
        same_ps = ps("same_ps", [P, 2 * BANK_COLS], FP32)
        place_ps = ps("place_ps", [P, 3 * BANK_COLS], FP32)
        misc_ps = ps("misc_ps", [P, BANK_COLS], FP32)

        src_loaded = sem("src_loaded")
        weights_loaded = sem("weights_loaded")
        x_loaded = sem("x_loaded")
        pad_written = sem("pad_written")
        const_made = sem("const_made")
        const_cast = sem("const_cast")
        split_done = sem("split_done")
        chunk_copied = sem("chunk_copied")
        count_hot = sem("count_hot")
        counted = sem("counted")
        offset_step = sem("offset_step")
        offset_pe = sem("offset_pe")
        passes_ready = sem("passes_ready")
        hot_ready = sem("hot_ready")
        hot_transposed = sem("hot_transposed")
        hot_copied = sem("hot_copied")
        same_ready = sem("same_ready")
        earlier_ready = sem("earlier_ready")
        start_copied = sem("start_copied")
        start_moved = sem("start_moved")
        place_ready = sem("place_ready")
        picked_sum = sem("picked_sum")
        position_ready = sem("position_ready")
        edges_loaded = [sem(f"edges_loaded{k}") for k in range(GROUPS)]
        edges_sent = [sem(f"edges_sent{k}") for k in range(GROUPS)]
        group_begun = sem("group_begun")
        windows_placed = sem("windows_placed")
        window_loaded = [sem(f"window_loaded{s}") for s in range(SLOTS)]
        masks_made = sem("masks_made")
        window_clipped = sem("window_clipped")
        window_masked = sem("window_masked")
        window_reduced = sem("window_reduced")
        round_added = sem("round_added")
        pass_moved = sem("pass_moved")
        mlp_prep = sem("mlp_prep")
        cat_ready = sem("cat_ready")
        cat_transposed = sem("cat_transposed")
        cat_copied = sem("cat_copied")
        hidden_summed = sem("hidden_summed")
        hidden_ready = sem("hidden_ready")
        out_summed = sem("out_summed")
        out_ready = sem("out_ready")
        out_written = sem("out_written")

        PLACE_BANK = [0, 1, 0, 1, 2]
        PLACE_USER = [3, 3, 2, 2, 5]

        def place_slot(j):
            return place_ps[:, PLACE_BANK[j] * BANK_COLS:PLACE_BANK[j] * BANK_COLS + P]

        block = ctx.enter_context(nc.Block())

        @block.sync
        def _(sp):
            sp.dma_start(src_i[:, :], src_view).then_inc(src_loaded, 16)
            sp.wait_ge(const_made, 3)
            sp.dma_start(rows[EDGES:EDGES + WINDOW, :].rearrange("(p r) f -> p (r f)", p=16),
                         zeros_f[0:16, :]).then_inc(pad_written, 16)
            sp.dma_start(w1_sb[:, :], w1[0:CAT, :]).then_inc(weights_loaded, 16)
            sp.dma_start(w1_u[:, :], w1[CAT, :].rearrange("(h o) -> h o", o=1)).then_inc(weights_loaded, 16)
            sp.dma_start(b1_sb[:, :], b1.rearrange("(h o) -> h o", o=1)).then_inc(weights_loaded, 16)
            sp.dma_start(u_sb[:, :], u[0:1, :].to_broadcast([HID, 1])).then_inc(weights_loaded, 16)
            sp.dma_start(w2_sb[:, :], w2[:, :]).then_inc(weights_loaded, 16)
            sp.dma_start(b2_sb[:, :], b2.rearrange("(o n) -> o n", o=1).to_broadcast([P, NODE_OUT]))\
                .then_inc(weights_loaded, 16)
            sp.wait_ge(const_cast, 5)
            sp.dma_start(x_sb[0:FULL_P, :], x[0:FULL_P * BLOCKS, :].rearrange("(p b) n -> p (b n)", b=BLOCKS))\
                .then_inc(x_loaded, 16)
            sp.dma_start(x_sb[FULL_P:FULL_P + 1, 0:REST * NODE_OUT],
                         x[FULL_P * BLOCKS:NODES, :].rearrange("(p b) n -> p (b n)", b=REST)).then_inc(x_loaded, 16)

            def load_group(c, k):
                at = (c * CHUNK + k * GROUP) * FEAT
                sp.dma_start(edges[:, k, :], edge_view[:, bass.ds(at, GROUP * FEAT)]).then_inc(edges_loaded[k], 16)

            for k in range(GROUPS):
                load_group(0, k)
            with sp.Fori(1, CHUNKS) as c:
                for k in range(GROUPS):
                    sp.wait_ge(edges_sent[k], c * (16 * GROUP))
                    load_group(c, k)
            sp.wait_ge(pad_written, 16)
            sp.wait_ge(out_ready, ROUNDS)
            sp.dma_start(out[0:FULL_P * BLOCKS, :].rearrange("(p b) n -> p (b n)", b=BLOCKS), x_sb[0:FULL_P, :])\
                .then_inc(out_written, 16)
            sp.dma_start(out[FULL_P * BLOCKS:NODES, :].rearrange("(p b) n -> p (b n)", b=REST),
                         x_sb[FULL_P:FULL_P + 1, 0:REST * NODE_OUT]).then_inc(out_written, 16)
            sp.wait_ge(out_written, 32)

        @block.gpsimd
        def _(pool):
            nc.gpsimd.memset(before_f[:, :], 1.0).then_inc(const_made, 1)
            nc.gpsimd.memset(ident_f[:, :], 0.0).then_inc(const_made, 1)
            nc.gpsimd.memset(zeros_f[:, :], 0.0).then_inc(const_made, 1)
            nc.gpsimd.iota(iota_i[:, :], pattern=[[1, P]], base=0, channel_multiplier=0).then_inc(const_made, 1)
            pool.wait_ge(const_made, 4)
            nc.gpsimd.affine_select(out=before_f[:, :], in_=before_f[:, :], compare_op=ALU.is_gt, fill=0.0,
                                    base=0, pattern=[[1, P]], channel_multiplier=-1).then_inc(const_made, 1)
            nc.gpsimd.affine_select(out=ident_f[:, :], in_=ident_f[:, :], compare_op=ALU.not_equal, fill=1.0,
                                    base=0, pattern=[[1, P]], channel_multiplier=-1).then_inc(const_made, 1)

            with pool.Fori(0, CHUNKS) as c:
                for k in range(GROUPS):
                    pool.wait_ge(position_ready, c * GROUPS + (k + 1))
                    pool.wait_ge(edges_loaded[k], c * 16 + 16)
                    pool.sem_inc(group_begun, 1)
                    for j in range(GROUP):
                        t = k * GROUP + j
                        nc.gpsimd.indirect_dma_start(
                            out=rows[:, :], out_offset=bass.IndirectOffsetOnAxis(ap=position[:, t:t + 1], axis=0),
                            in_=edges[:, k, j * FEAT:(j + 1) * FEAT], in_offset=None).then_inc(edges_sent[k], 16)
            for k in range(GROUPS):
                pool.wait_ge(edges_sent[k], CHUNKS * GROUP * 16)
            pool.wait_ge(pad_written, 16)
            pool.wait_ge(passes_ready, 1)
            passes = pool.value_load(passes_i[0:1, 0:1], min_val=1, max_val=-(-EDGES // WINDOW))
            with pool.Fori(0, passes * ROUNDS) as i:
                pool.wait_ge(windows_placed, i + 1)
                pool.sem_inc(group_begun, 1)
                for s in range(SLOTS):
                    nc.gpsimd.indirect_dma_start(
                        out=window[:, s, :], out_offset=None, in_=rows[:, :],
                        in_offset=bass.IndirectOffsetOnAxis(ap=window_at[:, s:s + 1], axis=0))\
                        .then_inc(window_loaded[s], 16)

        @block.tensor
        def _(pe):
            pe.wait_ge(const_cast, 5)
            nc.tensor.matmul(start_ps[0:BLOCKS, 0:P], zeros_b[:, 0:BLOCKS], zeros_b[:, :], start=True, stop=False)
            with pe.Fori(0, CHUNKS) as c:
                for g in range(GROUPS):
                    pe.wait_ge(count_hot, c * GROUPS + (g + 1))
                    for j in range(GROUP):
                        t = g * GROUP + j
                        last = nc.tensor.matmul(start_ps[0:BLOCKS, 0:P], hot_block[:, t, :], hot_owner[:, t, :],
                                                start=False, stop=False)
                    last.then_inc(counted, 1)
            nc.tensor.matmul(start_ps[0:BLOCKS, 0:P], zeros_b[:, 0:BLOCKS], zeros_b[:, :], start=False, stop=True)\
                .then_inc(counted, 1)

            pe.wait_ge(offset_step, 2)
            nc.tensor.matmul(misc_ps[0:BLOCKS, 0:1], before_f[0:BLOCKS, 0:BLOCKS], cumul[:, P - 1:P],
                             start=True, stop=True).then_inc(offset_pe, 1)
            pe.wait_ge(offset_step, 4)
            nc.tensor.matmul(start_ps[0:BLOCKS, 0:P], ident_f[0:BLOCKS, 0:BLOCKS], offset[:, :],
                             start=True, stop=False, skip_group_check=True).then_inc(start_moved, 1)
            nc.tensor.transpose(misc_ps[:, 128:128 + BLOCKS], offset[:, :], ident_f[0:BLOCKS, 0:BLOCKS])
            nc.tensor.transpose(misc_ps[:, 256:256 + BLOCKS], count[:, :], ident_f[0:BLOCKS, 0:BLOCKS])\
                .then_inc(offset_pe, 1)
            pe.wait_ge(offset_step, 7)
            nc.tensor.transpose(misc_ps[0:1, 0:P], most_p[:, :], ident_f[:, :]).then_inc(offset_pe, 1)

            def transpose_hot(n, g):
                pe.wait_ge(hot_ready, n + 1)
                for j in range(GROUP):
                    last = nc.tensor.transpose(hot_t_ps[0:BLOCKS, j * P:(j + 1) * P],
                                               hot_block[:, g * GROUP + j, :], ident_b[:, :])
                last.then_inc(hot_transposed, 1)

            def match_blocks(n, g):
                pe.wait_ge(hot_copied, n + 1)
                for j in range(GROUP):
                    hot = hot_block_t[:, g, j * P:(j + 1) * P]
                    last = nc.tensor.matmul(same_ps[:, j * P:(j + 1) * P], hot, hot, start=True, stop=True)
                last.then_inc(same_ready, 1)

            def place_group(n, g, first):
                pe.wait_ge(earlier_ready, n + 1)
                for j in range(GROUP):
                    t = g * GROUP + j
                    pe.wait_ge(start_copied, n * GROUP + (j + 1))
                    nc.tensor.matmul(start_ps[0:BLOCKS, 0:P], hot_block[:, t, :], hot_owner[:, t, :],
                                     start=False, stop=False, skip_group_check=True).then_inc(start_moved, 1)
                    if not first or PLACE_USER[j] <= j:
                        pe.wait_ge(picked_sum, n * GROUP + (j + 1 - PLACE_USER[j]))
                    nc.tensor.matmul(place_slot(j), hot_block_tf[:, g, j * P:(j + 1) * P], start_sb[:, j, :],
                                     start=True, stop=False)
                    nc.tensor.matmul(place_slot(j), earlier[:, g, j * P:(j + 1) * P], hot_owner[:, t, :],
                                     start=False, stop=True).then_inc(place_ready, 1)

            def step(c, g, first_chunk):
                n = c * GROUPS + g
                if not (first_chunk and g == 0):
                    pe.wait_ge(hot_copied, n)
                transpose_hot(n, g)
                if not (first_chunk and g < 2):
                    place_group(n - 2, (g - 2) % GROUPS, first_chunk and g == 2)
                if not (first_chunk and g == 0):
                    pe.wait_ge(earlier_ready, n)
                match_blocks(n, g)

            for g in range(GROUPS):
                step(0, g, True)
            with pe.Fori(1, CHUNKS) as c:
                for g in range(GROUPS):
                    step(c, g, False)
            for g in (GROUPS - 2, GROUPS - 1):
                place_group((CHUNKS - 1) * GROUPS + g, g, False)

            spans = [(0, 4), (4, SLOTS)]
            cat_banks = [same_ps[0:CAT, 0:BANK_COLS], same_ps[0:CAT, BANK_COLS:2 * BANK_COLS]]
            hid_banks = [place_ps[:, 0:BANK_COLS], place_ps[:, BANK_COLS:2 * BANK_COLS]]
            pe.wait_ge(mlp_prep, 4)
            with pe.Fori(0, ROUNDS) as r:
                pe.wait_ge(cat_ready, r + 1)
                for n, (a, z) in enumerate(spans):
                    for s in range(a, z):
                        last = nc.tensor.transpose(cat_banks[n][:, (s - a) * P:(s - a + 1) * P], cat[:, s, :],
                                                   ident_f[:, :])
                    last.then_inc(cat_transposed, 1)
                for n, (a, z) in enumerate(spans):
                    pe.wait_ge(cat_copied, 2 * r + (n + 1))
                    nc.tensor.matmul(hid_banks[n][:, 0:(z - a) * P], w1_sb[:, :], cat_t[:, a * P:z * P],
                                     start=True, stop=True).then_inc(hidden_summed, 1)
                for n, (a, z) in enumerate(spans):
                    pe.wait_ge(hidden_ready, 2 * r + (n + 1))
                    for s in range(a, z):
                        last = nc.tensor.matmul(misc_ps[:, s * NODE_OUT:(s + 1) * NODE_OUT],
                                                hidden[:, s * P:(s + 1) * P], w2_sb[:, :], start=True, stop=True)
                last.then_inc(out_summed, 1)

        @block.scalar
        def _(act):
            def copy_hot(n, g):
                act.wait_ge(hot_transposed, n + 1)
                nc.scalar.activation(hot_block_t[:, g, :], hot_t_ps[0:BLOCKS, 0:GROUP * P], ACT.Copy)
                nc.scalar.activation(hot_block_tf[:, g, :], hot_t_ps[0:BLOCKS, 0:GROUP * P], ACT.Copy)\
                    .then_inc(hot_copied, 1)

            def copy_starts(n, first):
                for j in range(GROUP):
                    act.wait_ge(start_moved, n * GROUP + (j + 1))
                    if not first:
                        act.wait_ge(place_ready, n * GROUP + (j + 1 - GROUP))
                    nc.scalar.activation(start_sb[:, j, :], start_ps[0:BLOCKS, 0:P], ACT.Copy)\
                        .then_inc(start_copied, 1)

            def step(c, g, first_chunk):
                n = c * GROUPS + g
                copy_hot(n, g)
                if not (first_chunk and g < 2):
                    copy_starts(n - 2, first_chunk and g == 2)

            for g in range(GROUPS):
                step(0, g, True)
            with act.Fori(1, CHUNKS) as c:
                for g in range(GROUPS):
                    step(c, g, False)
            for g in (GROUPS - 2, GROUPS - 1):
                copy_starts((CHUNKS - 1) * GROUPS + g, False)

            act.wait_ge(mlp_prep, 4)
            with act.Fori(0, ROUNDS) as r:
                for n, (a, z) in enumerate([(0, 4), (4, SLOTS)]):
                    act.wait_ge(cat_transposed, 2 * r + (n + 1))
                    nc.scalar.activation(cat_t[:, a * P:z * P], same_ps[0:CAT, n * BANK_COLS:n * BANK_COLS + (z - a) * P],
                                         ACT.Copy).then_inc(cat_copied, 1)
                for n, (a, z) in enumerate([(0, 4), (4, SLOTS)]):
                    act.wait_ge(hidden_summed, 2 * r + (n + 1))
                    nc.scalar.activation(hidden[:, a * P:z * P], place_ps[:, n * BANK_COLS:n * BANK_COLS + (z - a) * P],
                                         ACT.Relu, bias=bias1[:, 0:1]).then_inc(hidden_ready, 1)

        @block.vector
        def _(dve):
            nc.vector.memset(zeros_b[:, :], 0.0).then_inc(const_cast, 1)
            nc.vector.memset(x_sb[:, :], 0.0).then_inc(const_cast, 1)
            dve.wait_ge(const_made, 6)
            nc.vector.tensor_copy(iota_b[:, :], iota_i[:, :])
            nc.vector.tensor_copy(iota_f[:, :], iota_i[:, 0:WINDOW]).then_inc(const_cast, 1)
            nc.vector.tensor_copy(before_b[:, :], before_f[:, :]).then_inc(const_cast, 1)
            nc.vector.tensor_copy(ident_b[:, :], ident_f[:, :]).then_inc(const_cast, 1)
            dve.wait_ge(src_loaded, 16)
            nc.vector.tensor_copy(block_of, src_i[:, :]).then_inc(split_done, 1)
            dve.wait_ge(split_done, 1)
            nc.vector.tensor_scalar(src_i[:, :], block_of, -(BLOCKS - 1) / 2, 1.0 / BLOCKS, ALU.add, ALU.mult)\
                .then_inc(split_done, 1)
            dve.wait_ge(split_done, 2)
            nc.vector.tensor_copy(owner, src_i[:, :]).then_inc(split_done, 1)
            dve.wait_ge(split_done, 3)
            nc.vector.scalar_tensor_tensor(block_of, owner, -float(BLOCKS), block_of,
                                           ALU.mult, ALU.add).then_inc(split_done, 1)
            dve.wait_ge(split_done, 4)
            dve.wait_ge(const_cast, 5)

            def copy_chunk(c, copies):
                nc.vector.tensor_copy(owner_c[:, :], owner[:, bass.ds(c * CHUNK, CHUNK)])
                nc.vector.tensor_copy(block_c[:, :], block_of[:, bass.ds(c * CHUNK, CHUNK)]).then_inc(chunk_copied, 1)
                dve.wait_ge(chunk_copied, copies)

            def make_hot(g, done):
                for j in range(GROUP):
                    t = g * GROUP + j
                    nc.vector.tensor_scalar(hot_block[:, t, :], iota_b[:, 0:BLOCKS], block_c[:, t:t + 1], None,
                                            ALU.is_equal)
                    last = nc.vector.tensor_scalar(hot_owner[:, t, :], iota_b[:, :], owner_c[:, t:t + 1], None,
                                                   ALU.is_equal)
                last.then_inc(done, 1)

            copy_chunk(0, 1)
            for g in range(GROUPS):
                make_hot(g, count_hot)
            with dve.Fori(1, CHUNKS) as c:
                dve.wait_ge(count_hot, c * GROUPS)
                copy_chunk(c, c + 1)
                for g in range(GROUPS):
                    dve.wait_ge(counted, c * GROUPS + (g + 1 - GROUPS))
                    make_hot(g, count_hot)

            dve.wait_ge(counted, CHUNKS * GROUPS + 1)
            nc.vector.tensor_copy(count[:, :], start_ps[0:BLOCKS, 0:P]).then_inc(offset_step, 1)
            dve.wait_ge(offset_step, 1)
            nc.vector.tensor_tensor_scan(cumul[:, :], count[:, :], zeros_f[0:BLOCKS, :], 0.0, ALU.add, ALU.add)\
                .then_inc(offset_step, 1)
            dve.wait_ge(offset_pe, 1)
            dve.wait_ge(offset_step, 2)
            nc.vector.tensor_copy(block_base[:, :], misc_ps[0:BLOCKS, 0:1]).then_inc(offset_step, 1)
            dve.wait_ge(offset_step, 3)
            nc.vector.scalar_tensor_tensor(offset[:, :], cumul[:, :], block_base[:, 0:1], count[:, :],
                                           ALU.add, ALU.subtract).then_inc(offset_step, 1)
            dve.wait_ge(offset_pe, 2)
            nc.vector.tensor_copy(next_t[:, :], misc_ps[:, 128:128 + BLOCKS]).then_inc(offset_step, 1)
            nc.vector.tensor_copy(count_t[:, :], misc_ps[:, 256:256 + BLOCKS]).then_inc(offset_step, 1)
            dve.wait_ge(offset_step, 6)
            nc.vector.reduce_max(most_p[:, :], count_t[:, :], axis=AXIS_X).then_inc(offset_step, 1)
            nc.vector.tensor_copy(left_t[:, :], count_t[:, :]).then_inc(offset_step, 1)
            dve.wait_ge(offset_pe, 3)
            nc.vector.reduce_max(most[:, :], misc_ps[0:1, 0:P], axis=AXIS_X).then_inc(offset_step, 1)
            dve.wait_ge(offset_step, 9)
            nc.vector.tensor_scalar(passes_i[:, :], most[:, :], (WINDOW - 1) / 2, 1.0 / WINDOW, ALU.add, ALU.mult)\
                .then_inc(passes_ready, 1)

            def mark_earlier(n, g):
                dve.wait_ge(same_ready, n + 1)
                nc.vector.tensor_tensor(earlier[:, g, :].rearrange("p (j m) -> p j m", j=GROUP),
                                        same_ps[:, 0:GROUP * P].rearrange("p (j m) -> p j m", j=GROUP),
                                        before_b[:, :].unsqueeze(1).to_broadcast([P, GROUP, P]), ALU.mult)\
                    .then_inc(earlier_ready, 1)

            def pick_positions(c, g, n, first):
                for j in range(GROUP):
                    t = g * GROUP + j
                    dve.wait_ge(place_ready, n * GROUP + (j + 1))
                    nc.vector.tensor_tensor_reduce(out=picked[:, j, :], in0=place_slot(j), in1=hot_owner[:, t, :],
                                                   scale=1.0, scalar=0.0, op0=ALU.mult, op1=ALU.add,
                                                   accum_out=position_f[:, t:t + 1]).then_inc(picked_sum, 1)
                dve.wait_ge(picked_sum, (n + 1) * GROUP)
                if not first:
                    dve.wait_ge(edges_sent[g], c * (16 * GROUP))
                nc.vector.tensor_copy(position[:, g * GROUP:(g + 1) * GROUP], position_f[:, g * GROUP:(g + 1) * GROUP])\
                    .then_inc(position_ready, 1)

            def step(c, g, first_chunk):
                n = c * GROUPS + g
                make_hot(g, hot_ready)
                if not (first_chunk and g == 0):
                    mark_earlier(n - 1, (g - 1) % GROUPS)
                if not (first_chunk and g < 2):
                    if g < 2:
                        pick_positions(c - 1, (g - 2) % GROUPS, n - 2, False)
                    else:
                        pick_positions(c, g - 2, n - 2, first_chunk)

            dve.wait_ge(count_hot, CHUNKS * GROUPS)
            copy_chunk(0, CHUNKS + 1)
            for g in range(GROUPS):
                step(0, g, True)
            with dve.Fori(1, CHUNKS) as c:
                dve.wait_ge(hot_ready, c * GROUPS)
                copy_chunk(c, c + (CHUNKS + 1))
                for g in range(GROUPS):
                    step(c, g, False)
            last_group = CHUNKS * GROUPS - 1
            mark_earlier(last_group, GROUPS - 1)
            pick_positions(CHUNKS - 1, GROUPS - 2, last_group - 1, False)
            pick_positions(CHUNKS - 1, GROUPS - 1, last_group, False)

            nc.vector.memset(run_sum[:, :, :], 0.0)
            nc.vector.memset(run_max[:, :, :], -FLT_MAX).then_inc(round_added, 1)
            dve.wait_ge(round_added, 1)
            dve.wait_ge(passes_ready, 1)
            passes = dve.value_load(passes_i[0:1, 0:1], min_val=1, max_val=-(-EDGES // WINDOW))
            ahead = SLOTS * ROUNDS
            with dve.Fori(0, passes) as q:
                with dve.Fori(0, ROUNDS) as r:
                    i = q * ROUNDS + r
                    nc.vector.tensor_copy(window_at[:, :], next_t[:, bass.ds(r * SLOTS, SLOTS)])
                    nc.vector.tensor_copy(left_s[:, :], left_t[:, bass.ds(r * SLOTS, SLOTS)])\
                        .then_inc(windows_placed, 1)
                    dve.wait_ge(windows_placed, i + 1)
                    for s in range(SLOTS):
                        w = window[:, s, :]
                        k = i * SLOTS + s
                        nc.vector.tensor_scalar(half[:, :], iota_f[:, :], left_s[:, s:s + 1], 0.5,
                                                ALU.is_lt, ALU.subtract).then_inc(masks_made, 1)
                        dve.wait_ge(masks_made, k * 2 + 1)
                        nc.vector.tensor_scalar(bound[:, :], half[:, :], FLT_MAX, 2.0, ALU.mult, ALU.mult)
                        nc.vector.tensor_scalar(keep[:, :], half[:, :], 0.5, -1.0, ALU.add, ALU.mult)\
                            .then_inc(masks_made, 1)
                        dve.wait_ge(masks_made, k * 2 + 2)
                        dve.wait_ge(window_loaded[s], i * 16 + 16)
                        nc.vector.tensor_tensor(clipped[:, :].rearrange("p (r f) -> p r f", f=FEAT),
                                                w.rearrange("p (r f) -> p r f", f=FEAT),
                                                bound[:, :].unsqueeze(2).to_broadcast([P, WINDOW, FEAT]), ALU.min)\
                            .then_inc(window_clipped, 1)
                        nc.vector.tensor_tensor(w.bitcast(I32).rearrange("p (r f) -> p r f", f=FEAT),
                                                w.bitcast(I32).rearrange("p (r f) -> p r f", f=FEAT),
                                                keep[:, :].unsqueeze(2).to_broadcast([P, WINDOW, FEAT]),
                                                ALU.bitwise_and).then_inc(window_masked, 1)
                        dve.wait_ge(window_clipped, k + 1)
                        nc.vector.tensor_reduce(part_max[:, s, :], clipped[:, :].rearrange("p (r f) -> p f r", f=FEAT),
                                                AXIS_X, ALU.max)
                        dve.wait_ge(window_masked, k + 1)
                        nc.vector.tensor_reduce(part_sum[:, s, :], w.rearrange("p (r f) -> p f r", f=FEAT),
                                                AXIS_X, ALU.add).then_inc(window_reduced, 1)
                        dve.wait_ge(window_reduced, k + 1)
                    mine = bass.ds(r * SLOTS, SLOTS)
                    nc.vector.tensor_tensor(run_max[:, mine, :], run_max[:, mine, :], part_max[:, :, :], ALU.max)
                    nc.vector.tensor_tensor(run_sum[:, mine, :], run_sum[:, mine, :], part_sum[:, :, :], ALU.add)\
                        .then_inc(round_added, 1)
                    dve.wait_ge(round_added, i + 2)
                nc.vector.tensor_scalar(next_t[:, :], next_t[:, :], float(WINDOW), float(EDGES), ALU.add, ALU.min)
                nc.vector.tensor_scalar(left_t[:, :], left_t[:, :], float(WINDOW), None, ALU.subtract)\
                    .then_inc(pass_moved, 1)
                dve.wait_ge(pass_moved, q + 1)

            dve.wait_ge(weights_loaded, 6 * 16)
            dve.wait_ge(x_loaded, 32)
            nc.vector.tensor_scalar(divisor[:, :], count_t[:, :], 1.0, None, ALU.max).then_inc(mlp_prep, 1)
            nc.vector.tensor_scalar(nonempty[:, :], count_t[:, :], 0.0, None, ALU.is_gt).then_inc(mlp_prep, 1)
            nc.vector.scalar_tensor_tensor(bias1[:, :], w1_u[:, :], u_sb[:, 0:1], b1_sb[:, :], ALU.mult, ALU.add)\
                .then_inc(mlp_prep, 1)
            nc.vector.tensor_tensor(x_sb[:, :].rearrange("p (b n) -> p b n", n=NODE_OUT),
                                    x_sb[:, :].rearrange("p (b n) -> p b n", n=NODE_OUT),
                                    b2_sb[:, :].unsqueeze(1).to_broadcast([P, BLOCKS, NODE_OUT]), ALU.add)\
                .then_inc(mlp_prep, 1)
            dve.wait_ge(mlp_prep, 4)
            nc.vector.reciprocal(divisor[:, :], divisor[:, :]).then_inc(mlp_prep, 1)
            dve.wait_ge(mlp_prep, 5)
            with dve.Fori(0, ROUNDS) as r:
                mine = bass.ds(r * SLOTS, SLOTS)
                nc.vector.tensor_copy(cat[:, :, 0:FEAT], run_sum[:, mine, :])
                nc.vector.tensor_tensor(cat[:, :, FEAT:2 * FEAT], run_max[:, mine, :],
                                        nonempty[:, mine].unsqueeze(2).to_broadcast([P, SLOTS, FEAT]), ALU.mult)
                nc.vector.tensor_tensor(cat[:, :, 2 * FEAT:CAT], run_sum[:, mine, :],
                                        divisor[:, mine].unsqueeze(2).to_broadcast([P, SLOTS, FEAT]), ALU.mult)\
                    .then_inc(cat_ready, 1)
                dve.wait_ge(out_summed, r + 1)
                cols = bass.ds(r * (SLOTS * NODE_OUT), SLOTS * NODE_OUT)
                nc.vector.tensor_tensor(x_sb[:, cols], x_sb[:, cols], misc_ps[:, 0:SLOTS * NODE_OUT], ALU.add)\
                    .then_inc(out_ready, 1)
                dve.wait_ge(out_ready, r + 1)


def kernel(x, src, dst, edge_attr_32, L0_gnn_u, L0_gnn_W1, L0_gnn_b1, L0_gnn_W2, L0_gnn_b2):
    import concourse.bacc as bacc
    from concourse.bass_utils import run_bass_kernel_spmd

    nc = bacc.Bacc("TRN2", target_bir_lowering=False, num_devices=1)
    given = {"x": x, "src": src, "edge_attr": edge_attr_32, "u": L0_gnn_u, "w1": L0_gnn_W1, "b1": L0_gnn_b1,
             "w2": L0_gnn_W2, "b2": L0_gnn_b2}
    arrays, aps = {}, {}
    for name, value in given.items():
        a = np.ascontiguousarray(value)
        arrays[f"in_{name}"] = a
        aps[name] = nc.dram_tensor(f"in_{name}", a.shape, mybir.dt.from_np(a.dtype), kind="ExternalInput").ap()
    edges, feat = aps["edge_attr"].shape
    out = nc.dram_tensor("out", aps["x"].shape, FP32, kind="ExternalOutput").ap()
    rows = nc.dram_tensor("sorted_rows", (edges + 64, feat), FP32, kind="Internal").ap()
    build(nc, aps["x"], aps["src"], aps["edge_attr"], aps["u"], aps["w1"], aps["b1"], aps["w2"], aps["b2"], out, rows)
    r = run_bass_kernel_spmd(nc, [arrays], core_ids=[0])
    return r.results[0]["out"]
```

```python
from contextlib import ExitStack

import numpy as np

import concourse.bass as bass
from concourse import mybir

FP32 = mybir.dt.float32
BF16 = mybir.dt.bfloat16
I32 = mybir.dt.int32
ALU = mybir.AluOpType
ACT = mybir.ActivationFunctionType
AXIS_X = mybir.AxisListType.X
FLT_MAX = float(np.finfo(np.float32).max)


def build(nc, x, src, edge_attr, u, w1, b1, w2, b2, out, rows):
    P = 128
    EDGES, FEAT = edge_attr.shape
    NODES, NODE_OUT = x.shape
    HID = w1.shape[1]
    BLOCKS = -(-NODES // P)
    TILES = EDGES // P
    GROUP = 5
    GROUPS = 5
    CHUNK = GROUP * GROUPS
    CHUNKS = TILES // CHUNK
    assert EDGES == P * CHUNK * CHUNKS
    WINDOW = 64
    SLOTS = 7
    ROUNDS = BLOCKS // SLOTS
    assert ROUNDS * SLOTS == BLOCKS
    CAT = 3 * FEAT
    FULL_P = NODES // BLOCKS
    REST = NODES - FULL_P * BLOCKS
    BANK_COLS = 512

    src_view = src.rearrange("(p t) -> p t", p=P)
    edge_view = edge_attr.rearrange("(p t) f -> p (t f)", p=P)

    ctx = ExitStack()
    with ctx:
        def sb(name, shape, dt):
            return ctx.enter_context(nc.sbuf_tensor(name, shape, dt))

        def ps(name, shape, dt):
            return ctx.enter_context(nc.psum_tensor(name, shape, dt))

        def sem(name):
            return ctx.enter_context(nc.semaphore(name))

        iota_i = sb("iota_i", [P, P], I32)
        iota_b = sb("iota_b", [P, P], BF16)
        iota_f = sb("iota_f", [P, WINDOW], FP32)
        before_f = sb("before_f", [P, P], FP32)
        before_b = sb("before_b", [P, P], BF16)
        ident_f = sb("ident_f", [P, P], FP32)
        ident_b = sb("ident_b", [P, P], BF16)
        zeros_b = sb("zeros_b", [P, P], BF16)
        zeros_f = sb("zeros_f", [P, P], FP32)
        src_i = sb("src_i", [P, TILES], I32)
        run_sum = sb("run_sum", [P, BLOCKS, FEAT], FP32)
        run_max = sb("run_max", [P, BLOCKS, FEAT], FP32)
        owner = run_sum[:, :, :].rearrange("p b f -> p (b f)")[:, 0:TILES]
        block_of = run_max[:, :, :].rearrange("p b f -> p (b f)")[:, 0:TILES]
        x_sb = sb("x_sb", [P, BLOCKS * NODE_OUT], FP32)
        ids_2 = x_sb[:, :].bitcast(BF16)
        owner_2 = ids_2[:, 0:2 * TILES].rearrange("p (t w) -> p t w", w=2)
        block_2 = ids_2[:, BLOCKS * NODE_OUT:BLOCKS * NODE_OUT + 2 * TILES].rearrange("p (t w) -> p t w", w=2)
        owner_c = sb("owner_c", [P, CHUNK, 2], BF16)
        block_c = sb("block_c", [P, CHUNK, 2], BF16)
        hot_block = sb("hot_block", [P, CHUNK, BLOCKS], BF16)
        hot_owner = sb("hot_owner", [P, CHUNK, P], BF16)
        hot_block_t = sb("hot_block_t", [BLOCKS, GROUPS, GROUP * P], BF16)
        hot_block_tf = sb("hot_block_tf", [BLOCKS, GROUPS, GROUP * P], FP32)
        earlier = sb("earlier", [P, GROUPS, GROUP * P], BF16)
        start_sb = sb("start_sb", [BLOCKS, GROUP, P], FP32)
        picked = sb("picked", [P, GROUP, P], BF16)
        position_f = sb("position_f", [P, CHUNK], FP32)
        position = sb("position", [P, CHUNK], I32)
        edges = sb("edges", [P, GROUPS, GROUP * FEAT], FP32)
        count = sb("count", [BLOCKS, P], FP32)
        cumul = sb("cumul", [BLOCKS, P], FP32)
        block_base = sb("block_base", [BLOCKS, 1], FP32)
        offset = sb("offset", [BLOCKS, P], FP32)
        count_t = sb("count_t", [P, BLOCKS], FP32)
        left_t = sb("left_t", [P, BLOCKS], FP32)
        next_t = sb("next_t", [P, BLOCKS], FP32)
        most_p = sb("most_p", [P, 1], FP32)
        most = sb("most", [1, 1], FP32)
        passes_i = sb("passes_i", [1, 1], I32)
        window = sb("window", [P, SLOTS, WINDOW * FEAT], FP32)
        clipped = sb("clipped", [P, WINDOW * FEAT], FP32)
        window_at = sb("window_at", [P, SLOTS], I32)
        left_s = sb("left_s", [P, SLOTS], FP32)
        half = sb("half", [P, WINDOW], FP32)
        bound = sb("bound", [P, WINDOW], FP32)
        keep = sb("keep", [P, WINDOW], I32)
        part_sum = sb("part_sum", [P, SLOTS, FEAT], FP32)
        part_max = sb("part_max", [P, SLOTS, FEAT], FP32)
        divisor = sb("divisor", [P, BLOCKS], FP32)
        nonempty = sb("nonempty", [P, BLOCKS], FP32)
        w1_sb = sb("w1_sb", [CAT, HID], FP32)
        w1_u = sb("w1_u", [HID, 1], FP32)
        b1_sb = sb("b1_sb", [HID, 1], FP32)
        u_sb = sb("u_sb", [HID, 1], FP32)
        bias1 = sb("bias1", [HID, 1], FP32)
        w2_sb = sb("w2_sb", [HID, NODE_OUT], FP32)
        b2_sb = sb("b2_sb", [P, NODE_OUT], FP32)
        cat = sb("cat", [P, SLOTS, CAT], FP32)
        cat_t = sb("cat_t", [CAT, SLOTS * P], FP32)
        hidden = sb("hidden", [HID, SLOTS * P], FP32)

        start_ps = ps("start_ps", [P, BANK_COLS], FP32)
        hot_t_ps = ps("hot_t_ps", [P, 2 * BANK_COLS], BF16)
        same_ps = ps("same_ps", [P, 2 * BANK_COLS], FP32)
        place_ps = ps("place_ps", [P, 3 * BANK_COLS], FP32)
        misc_ps = ps("misc_ps", [P, BANK_COLS], FP32)

        src_loaded = sem("src_loaded")
        weights_loaded = sem("weights_loaded")
        x_cleared = sem("x_cleared")
        x_loaded = sem("x_loaded")
        pad_written = sem("pad_written")
        const_made = sem("const_made")
        const_cast = sem("const_cast")
        split_done = sem("split_done")
        chunk_copied = sem("chunk_copied")
        count_hot = sem("count_hot")
        counted = sem("counted")
        offset_step = sem("offset_step")
        offset_pe = sem("offset_pe")
        passes_ready = sem("passes_ready")
        hot_ready = sem("hot_ready")
        hot_transposed = sem("hot_transposed")
        hot_copied = sem("hot_copied")
        hot_cast = sem("hot_cast")
        same_ready = sem("same_ready")
        earlier_ready = sem("earlier_ready")
        start_copied = sem("start_copied")
        start_moved = sem("start_moved")
        place_ready = sem("place_ready")
        picked_sum = sem("picked_sum")
        position_ready = sem("position_ready")
        edges_loaded = [sem(f"edges_loaded{k}") for k in range(GROUPS)]
        edges_sent = [sem(f"edges_sent{k}") for k in range(GROUPS)]
        group_begun = sem("group_begun")
        windows_placed = sem("windows_placed")
        window_loaded = [sem(f"window_loaded{s}") for s in range(SLOTS)]
        masks_made = sem("masks_made")
        window_clipped = sem("window_clipped")
        window_masked = sem("window_masked")
        window_reduced = sem("window_reduced")
        round_added = sem("round_added")
        pass_moved = sem("pass_moved")
        mlp_prep = sem("mlp_prep")
        cat_ready = sem("cat_ready")
        cat_transposed = sem("cat_transposed")
        cat_copied = sem("cat_copied")
        hidden_summed = sem("hidden_summed")
        hidden_ready = sem("hidden_ready")
        out_summed = sem("out_summed")
        out_ready = sem("out_ready")
        out_written = sem("out_written")

        PLACE_BANK = [0, 1, 0, 1, 2]
        PLACE_USER = [3, 3, 2, 2, 5]

        COUNT_SPANS = [(0, CHUNK // 2), (CHUNK // 2, CHUNK)]

        LAG_TRANSPOSE, LAG_SAME, LAG_EARLIER, LAG_PLACE = 1, 2, 3, 4
        LAST_STEP = CHUNKS * GROUPS - 1 + LAG_PLACE
        HALF = 2 * P
        BANK_TILES = BANK_COLS // P

        def has(n, lag):
            return not isinstance(n, int) or lag <= n < CHUNKS * GROUPS + lag

        def place_slot(j):
            return place_ps[:, PLACE_BANK[j] * BANK_COLS:PLACE_BANK[j] * BANK_COLS + P]

        block = ctx.enter_context(nc.Block())

        @block.sync
        def _(sp):
            sp.dma_start(src_i[:, :], src_view).then_inc(src_loaded, 16)
            sp.wait_ge(const_made, 3)
            sp.dma_start(rows[EDGES:EDGES + WINDOW, :].rearrange("(p r) f -> p (r f)", p=16),
                         zeros_f[0:16, :]).then_inc(pad_written, 16)
            sp.dma_start(w1_sb[:, :], w1[0:CAT, :]).then_inc(weights_loaded, 16)
            sp.dma_start(w1_u[:, :], w1[CAT, :].rearrange("(h o) -> h o", o=1)).then_inc(weights_loaded, 16)
            sp.dma_start(b1_sb[:, :], b1.rearrange("(h o) -> h o", o=1)).then_inc(weights_loaded, 16)
            sp.dma_start(u_sb[:, :], u[0:1, :].to_broadcast([HID, 1])).then_inc(weights_loaded, 16)
            sp.dma_start(w2_sb[:, :], w2[:, :]).then_inc(weights_loaded, 16)
            sp.dma_start(b2_sb[:, :], b2.rearrange("(o n) -> o n", o=1).to_broadcast([P, NODE_OUT]))\
                .then_inc(weights_loaded, 16)

            def load_group(c, k):
                at = (c * CHUNK + k * GROUP) * FEAT
                sp.dma_start(edges[:, k, :], edge_view[:, bass.ds(at, GROUP * FEAT)]).then_inc(edges_loaded[k], 16)

            for k in range(GROUPS):
                load_group(0, k)
            with sp.Fori(1, CHUNKS) as c:
                for k in range(GROUPS):
                    sp.wait_ge(edges_sent[k], c * (16 * GROUP))
                    load_group(c, k)
            sp.wait_ge(x_cleared, 1)
            sp.dma_start(x_sb[0:FULL_P, :], x[0:FULL_P * BLOCKS, :].rearrange("(p b) n -> p (b n)", b=BLOCKS))\
                .then_inc(x_loaded, 16)
            sp.dma_start(x_sb[FULL_P:FULL_P + 1, 0:REST * NODE_OUT],
                         x[FULL_P * BLOCKS:NODES, :].rearrange("(p b) n -> p (b n)", b=REST)).then_inc(x_loaded, 16)
            sp.wait_ge(pad_written, 16)
            sp.wait_ge(out_ready, ROUNDS)
            sp.dma_start(out[0:FULL_P * BLOCKS, :].rearrange("(p b) n -> p (b n)", b=BLOCKS), x_sb[0:FULL_P, :])\
                .then_inc(out_written, 16)
            sp.dma_start(out[FULL_P * BLOCKS:NODES, :].rearrange("(p b) n -> p (b n)", b=REST),
                         x_sb[FULL_P:FULL_P + 1, 0:REST * NODE_OUT]).then_inc(out_written, 16)
            sp.wait_ge(out_written, 32)

        @block.gpsimd
        def _(pool):
            nc.gpsimd.memset(before_f[:, :], 1.0).then_inc(const_made, 1)
            nc.gpsimd.memset(ident_f[:, :], 0.0).then_inc(const_made, 1)
            nc.gpsimd.memset(zeros_f[:, :], 0.0).then_inc(const_made, 1)
            nc.gpsimd.iota(iota_i[:, :], pattern=[[1, P]], base=0, channel_multiplier=0).then_inc(const_made, 1)
            pool.wait_ge(const_made, 4)
            nc.gpsimd.affine_select(out=before_f[:, :], in_=before_f[:, :], compare_op=ALU.is_gt, fill=0.0,
                                    base=0, pattern=[[1, P]], channel_multiplier=-1).then_inc(const_made, 1)
            nc.gpsimd.affine_select(out=ident_f[:, :], in_=ident_f[:, :], compare_op=ALU.not_equal, fill=1.0,
                                    base=0, pattern=[[1, P]], channel_multiplier=-1).then_inc(const_made, 1)

            with pool.Fori(0, CHUNKS) as c:
                for k in range(GROUPS):
                    pool.wait_ge(position_ready, c * GROUPS + (k + 1))
                    pool.wait_ge(edges_loaded[k], c * 16 + 16)
                    pool.sem_inc(group_begun, 1)
                    for j in range(GROUP):
                        t = k * GROUP + j
                        nc.gpsimd.indirect_dma_start(
                            out=rows[:, :], out_offset=bass.IndirectOffsetOnAxis(ap=position[:, t:t + 1], axis=0),
                            in_=edges[:, k, j * FEAT:(j + 1) * FEAT], in_offset=None).then_inc(edges_sent[k], 16)
            for k in range(GROUPS):
                pool.wait_ge(edges_sent[k], CHUNKS * GROUP * 16)
            pool.wait_ge(pad_written, 16)
            pool.wait_ge(passes_ready, 1)
            passes = pool.value_load(passes_i[0:1, 0:1], min_val=1, max_val=-(-EDGES // WINDOW))
            with pool.Fori(0, passes * ROUNDS) as i:
                pool.wait_ge(windows_placed, i + 1)
                pool.sem_inc(group_begun, 1)
                for s in range(SLOTS):
                    nc.gpsimd.indirect_dma_start(
                        out=window[:, s, :], out_offset=None, in_=rows[:, :],
                        in_offset=bass.IndirectOffsetOnAxis(ap=window_at[:, s:s + 1], axis=0))\
                        .then_inc(window_loaded[s], 16)

        @block.tensor
        def _(pe):
            pe.wait_ge(const_cast, 4)
            nc.tensor.matmul(start_ps[0:BLOCKS, 0:P], zeros_b[:, 0:BLOCKS], zeros_b[:, :], start=True, stop=False)
            with pe.Fori(0, CHUNKS) as c:
                for k, (a, z) in enumerate(COUNT_SPANS):
                    pe.wait_ge(count_hot, c * 2 + (k + 1))
                    for t in range(a, z):
                        last = nc.tensor.matmul(start_ps[0:BLOCKS, 0:P], hot_block[:, t, :], hot_owner[:, t, :],
                                                start=False, stop=False)
                    last.then_inc(counted, 1)
            nc.tensor.matmul(start_ps[0:BLOCKS, 0:P], zeros_b[:, 0:BLOCKS], zeros_b[:, :], start=False, stop=True)\
                .then_inc(counted, 1)

            pe.wait_ge(offset_step, 2)
            nc.tensor.matmul(misc_ps[0:BLOCKS, 0:1], before_f[0:BLOCKS, 0:BLOCKS], cumul[:, P - 1:P],
                             start=True, stop=True).then_inc(offset_pe, 1)
            pe.wait_ge(offset_step, 4)
            nc.tensor.matmul(start_ps[0:BLOCKS, 0:P], ident_f[0:BLOCKS, 0:BLOCKS], offset[:, :],
                             start=True, stop=False, skip_group_check=True).then_inc(start_moved, 1)
            nc.tensor.transpose(misc_ps[:, 128:128 + BLOCKS], offset[:, :], ident_f[0:BLOCKS, 0:BLOCKS])
            nc.tensor.transpose(misc_ps[:, 256:256 + BLOCKS], count[:, :], ident_f[0:BLOCKS, 0:BLOCKS])\
                .then_inc(offset_pe, 1)
            pe.wait_ge(offset_step, 7)
            nc.tensor.transpose(misc_ps[0:1, 0:P], most_p[:, :], ident_f[:, :]).then_inc(offset_pe, 1)

            def transpose_tile(m, slot, j):
                if j == 0:
                    pe.wait_ge(hot_ready, m + 1)
                    if not isinstance(m, int) or m > 0:
                        pe.wait_ge(hot_copied, m)
                last = nc.tensor.transpose(hot_t_ps[0:BLOCKS, j * P:(j + 1) * P],
                                           hot_block[:, slot * GROUP + j, :], ident_b[:, :])
                if j == GROUP - 1:
                    last.then_inc(hot_transposed, 1)

            def match_tile(m, slot, j):
                if j == 0:
                    pe.wait_ge(hot_cast, m + 1)
                if j in (0, BANK_TILES) and (not isinstance(m, int) or m > 0):
                    pe.wait_ge(earlier_ready, m * 2 - (1 if j == 0 else 0))
                hot = hot_block_t[:, slot, j * P:(j + 1) * P]
                last = nc.tensor.matmul(same_ps[:, j * P:(j + 1) * P], hot, hot, start=True, stop=True)
                if j in (BANK_TILES - 1, GROUP - 1):
                    last.then_inc(same_ready, 1)

            def place_tile(m, slot, j):
                t = slot * GROUP + j
                if j == 0:
                    pe.wait_ge(earlier_ready, m * 2 + 2)
                pe.wait_ge(start_copied, m * GROUP + (j + 1))
                nc.tensor.matmul(start_ps[0:BLOCKS, 0:P], hot_block[:, t, :], hot_owner[:, t, :],
                                 start=False, stop=False, skip_group_check=True).then_inc(start_moved, 1)
                if not isinstance(m, int) or m * GROUP + j >= PLACE_USER[j]:
                    pe.wait_ge(picked_sum, m * GROUP + (j + 1 - PLACE_USER[j]))
                nc.tensor.matmul(place_slot(j), hot_block_tf[:, slot, j * P:(j + 1) * P], start_sb[:, j, :],
                                 start=True, stop=False)
                nc.tensor.matmul(place_slot(j), earlier[:, slot, j * P:(j + 1) * P], hot_owner[:, t, :],
                                 start=False, stop=True).then_inc(place_ready, 1)

            def step(n, g):
                fill = []
                if has(n, LAG_TRANSPOSE):
                    fill += [(transpose_tile, LAG_TRANSPOSE, j) for j in range(GROUP)]
                if has(n, LAG_SAME):
                    fill += [(match_tile, LAG_SAME, j) for j in range(GROUP)]
                for j in range(GROUP):
                    if has(n, LAG_PLACE):
                        place_tile(n - LAG_PLACE, (g - LAG_PLACE) % GROUPS, j)
                    for work, lag, k in fill[2 * j:2 * j + 2]:
                        work(n - lag, (g - lag) % GROUPS, k)

            for n in range(GROUPS):
                step(n, n)
            with pe.Fori(1, CHUNKS) as c:
                for g in range(GROUPS):
                    step(c * GROUPS + g, g)
            for n in range(CHUNKS * GROUPS, LAST_STEP + 1):
                step(n, n % GROUPS)

            spans = [(0, 4), (4, SLOTS)]
            cat_banks = [same_ps[0:CAT, 0:BANK_COLS], same_ps[0:CAT, BANK_COLS:2 * BANK_COLS]]
            hid_banks = [place_ps[:, 0:BANK_COLS], place_ps[:, BANK_COLS:2 * BANK_COLS]]
            pe.wait_ge(mlp_prep, 4)
            with pe.Fori(0, ROUNDS) as r:
                pe.wait_ge(cat_ready, r + 1)
                for n, (a, z) in enumerate(spans):
                    for s in range(a, z):
                        last = nc.tensor.transpose(cat_banks[n][:, (s - a) * P:(s - a + 1) * P], cat[:, s, :],
                                                   ident_f[:, :])
                    last.then_inc(cat_transposed, 1)
                for n, (a, z) in enumerate(spans):
                    pe.wait_ge(cat_copied, 2 * r + (n + 1))
                    nc.tensor.matmul(hid_banks[n][:, 0:(z - a) * P], w1_sb[:, :], cat_t[:, a * P:z * P],
                                     start=True, stop=True).then_inc(hidden_summed, 1)
                for n, (a, z) in enumerate(spans):
                    pe.wait_ge(hidden_ready, 2 * r + (n + 1))
                    for s in range(a, z):
                        last = nc.tensor.matmul(misc_ps[:, s * NODE_OUT:(s + 1) * NODE_OUT],
                                                hidden[:, s * P:(s + 1) * P], w2_sb[:, :], start=True, stop=True)
                last.then_inc(out_summed, 1)

        @block.scalar
        def _(act):
            def copy_start(m, j):
                act.wait_ge(start_moved, m * GROUP + (j + 1))
                if not isinstance(m, int) or m > 0:
                    act.wait_ge(place_ready, m * GROUP + (j + 1 - GROUP))
                nc.scalar.activation(start_sb[:, j, :], start_ps[0:BLOCKS, 0:P], ACT.Copy).then_inc(start_copied, 1)

            def step(n, g):
                slot = (g - LAG_TRANSPOSE) % GROUPS
                for j in range(GROUP):
                    if has(n, LAG_PLACE):
                        copy_start(n - LAG_PLACE, j)
                    if j == 3 and has(n, LAG_TRANSPOSE):
                        act.wait_ge(hot_transposed, n - LAG_TRANSPOSE + 1)
                        nc.scalar.activation(hot_block_tf[:, slot, 0:HALF], hot_t_ps[0:BLOCKS, 0:HALF], ACT.Copy)
                if has(n, LAG_TRANSPOSE):
                    nc.scalar.activation(hot_block_tf[:, slot, HALF:], hot_t_ps[0:BLOCKS, HALF:GROUP * P], ACT.Copy)\
                        .then_inc(hot_copied, 1)

            for n in range(GROUPS):
                step(n, n)
            with act.Fori(1, CHUNKS) as c:
                for g in range(GROUPS):
                    step(c * GROUPS + g, g)
            for n in range(CHUNKS * GROUPS, LAST_STEP + 1):
                step(n, n % GROUPS)

            act.wait_ge(mlp_prep, 4)
            with act.Fori(0, ROUNDS) as r:
                for n, (a, z) in enumerate([(0, 4), (4, SLOTS)]):
                    act.wait_ge(cat_transposed, 2 * r + (n + 1))
                    nc.scalar.activation(cat_t[:, a * P:z * P], same_ps[0:CAT, n * BANK_COLS:n * BANK_COLS + (z - a) * P],
                                         ACT.Copy).then_inc(cat_copied, 1)
                for n, (a, z) in enumerate([(0, 4), (4, SLOTS)]):
                    act.wait_ge(hidden_summed, 2 * r + (n + 1))
                    nc.scalar.activation(hidden[:, a * P:z * P], place_ps[:, n * BANK_COLS:n * BANK_COLS + (z - a) * P],
                                         ACT.Relu, bias=bias1[:, 0:1]).then_inc(hidden_ready, 1)

        @block.vector
        def _(dve):
            nc.vector.memset(zeros_b[:, :], 0.0).then_inc(const_cast, 1)
            dve.wait_ge(const_made, 6)
            nc.vector.tensor_copy(iota_b[:, :], iota_i[:, :])
            nc.vector.tensor_copy(iota_f[:, :], iota_i[:, 0:WINDOW]).then_inc(const_cast, 1)
            nc.vector.tensor_copy(before_b[:, :], before_f[:, :]).then_inc(const_cast, 1)
            nc.vector.tensor_copy(ident_b[:, :], ident_f[:, :]).then_inc(const_cast, 1)
            dve.wait_ge(src_loaded, 16)
            nc.vector.tensor_copy(block_of, src_i[:, :]).then_inc(split_done, 1)
            dve.wait_ge(split_done, 1)
            nc.vector.tensor_scalar(src_i[:, :], block_of, -(BLOCKS - 1) / 2, 1.0 / BLOCKS, ALU.add, ALU.mult)\
                .then_inc(split_done, 1)
            dve.wait_ge(split_done, 2)
            nc.vector.tensor_copy(owner, src_i[:, :]).then_inc(split_done, 1)
            dve.wait_ge(split_done, 3)
            nc.vector.scalar_tensor_tensor(block_of, owner, -float(BLOCKS), block_of,
                                           ALU.mult, ALU.add).then_inc(split_done, 1)
            dve.wait_ge(split_done, 4)
            nc.vector.tensor_copy(owner_2, owner.unsqueeze(2).to_broadcast([P, TILES, 2]))
            nc.vector.tensor_copy(block_2, block_of.unsqueeze(2).to_broadcast([P, TILES, 2]))\
                .then_inc(split_done, 1)
            dve.wait_ge(split_done, 5)
            dve.wait_ge(const_cast, 4)

            def copy_chunk(c, copies):
                nc.vector.tensor_copy(owner_c[:, :, :], owner_2[:, bass.ds(c * CHUNK, CHUNK), :])
                nc.vector.tensor_copy(block_c[:, :, :], block_2[:, bass.ds(c * CHUNK, CHUNK), :])\
                    .then_inc(chunk_copied, 1)
                dve.wait_ge(chunk_copied, copies)

            def make_hot(hot, ids, values, a, z):
                pairs = values // 2
                return nc.vector.tensor_tensor(
                    hot[:, a:z, :].rearrange("p t (v w) -> p t v w", w=2),
                    ids[:, a:z, :].unsqueeze(2).to_broadcast([P, z - a, pairs, 2]),
                    iota_b[:, 0:values].rearrange("p (v w) -> p v w", w=2).unsqueeze(1)
                    .to_broadcast([P, z - a, pairs, 2]), ALU.is_equal)

            def count_chunk(c):
                for k, (a, z) in enumerate(COUNT_SPANS):
                    if not isinstance(c, int):
                        dve.wait_ge(counted, c * 2 + (k - 1))
                    make_hot(hot_block, block_c, BLOCKS, a, z)
                    make_hot(hot_owner, owner_c, P, a, z).then_inc(count_hot, 1)

            copy_chunk(0, 1)
            count_chunk(0)
            with dve.Fori(1, CHUNKS) as c:
                dve.wait_ge(count_hot, c * 2)
                copy_chunk(c, c + 1)
                count_chunk(c)

            dve.wait_ge(counted, CHUNKS * 2 + 1)
            nc.vector.tensor_copy(count[:, :], start_ps[0:BLOCKS, 0:P]).then_inc(offset_step, 1)
            dve.wait_ge(offset_step, 1)
            nc.vector.tensor_tensor_scan(cumul[:, :], count[:, :], zeros_f[0:BLOCKS, :], 0.0, ALU.add, ALU.add)\
                .then_inc(offset_step, 1)
            dve.wait_ge(offset_pe, 1)
            dve.wait_ge(offset_step, 2)
            nc.vector.tensor_copy(block_base[:, :], misc_ps[0:BLOCKS, 0:1]).then_inc(offset_step, 1)
            dve.wait_ge(offset_step, 3)
            nc.vector.scalar_tensor_tensor(offset[:, :], cumul[:, :], block_base[:, 0:1], count[:, :],
                                           ALU.add, ALU.subtract).then_inc(offset_step, 1)
            dve.wait_ge(offset_pe, 2)
            nc.vector.tensor_copy(next_t[:, :], misc_ps[:, 128:128 + BLOCKS]).then_inc(offset_step, 1)
            nc.vector.tensor_copy(count_t[:, :], misc_ps[:, 256:256 + BLOCKS]).then_inc(offset_step, 1)
            dve.wait_ge(offset_step, 6)
            nc.vector.reduce_max(most_p[:, :], count_t[:, :], axis=AXIS_X).then_inc(offset_step, 1)
            nc.vector.tensor_copy(left_t[:, :], count_t[:, :]).then_inc(offset_step, 1)
            dve.wait_ge(offset_pe, 3)
            nc.vector.reduce_max(most[:, :], misc_ps[0:1, 0:P], axis=AXIS_X).then_inc(offset_step, 1)
            dve.wait_ge(offset_step, 9)
            nc.vector.tensor_scalar(passes_i[:, :], most[:, :], (WINDOW - 1) / 2, 1.0 / WINDOW, ALU.add, ALU.mult)\
                .then_inc(passes_ready, 1)

            def cast_hot(m, slot):
                dve.wait_ge(hot_copied, m + 1)
                nc.vector.tensor_copy(hot_block_t[:, slot, :], hot_block_tf[:, slot, :]).then_inc(hot_cast, 1)

            def mark_earlier(m, slot, part):
                a, z = ((0, BANK_TILES), (BANK_TILES, GROUP))[part]
                dve.wait_ge(same_ready, m * 2 + (part + 1))
                nc.vector.tensor_tensor(earlier[:, slot, a * P:z * P].rearrange("p (j m) -> p j m", j=z - a),
                                        same_ps[:, a * P:z * P].rearrange("p (j m) -> p j m", j=z - a),
                                        before_b[:, :].unsqueeze(1).to_broadcast([P, z - a, P]), ALU.mult)\
                    .then_inc(earlier_ready, 1)

            def pick_position(m, slot, j):
                t = slot * GROUP + j
                dve.wait_ge(place_ready, m * GROUP + (j + 1))
                nc.vector.tensor_tensor_reduce(out=picked[:, j, :], in0=place_slot(j), in1=hot_owner[:, t, :],
                                               scale=1.0, scalar=0.0, op0=ALU.mult, op1=ALU.add,
                                               accum_out=position_f[:, t:t + 1]).then_inc(picked_sum, 1)

            def cast_positions(m, slot, sent):
                dve.wait_ge(picked_sum, m * GROUP + GROUP)
                if not isinstance(m, int) or m >= GROUPS:
                    dve.wait_ge(edges_sent[slot], sent * (16 * GROUP))
                mine = slice(slot * GROUP, (slot + 1) * GROUP)
                nc.vector.tensor_copy(position[:, mine], position_f[:, mine]).then_inc(position_ready, 1)

            def step(c, n, g):
                if has(n, LAG_SAME):
                    cast_hot(n - LAG_SAME, (g - LAG_SAME) % GROUPS)
                place, slot = n - LAG_PLACE, (g - LAG_PLACE) % GROUPS
                for j in range(GROUP):
                    if has(n, LAG_PLACE):
                        pick_position(place, slot, j)
                    if j in (0, 1) and has(n, LAG_EARLIER):
                        mark_earlier(n - LAG_EARLIER, (g - LAG_EARLIER) % GROUPS, j)
                    if j in (2, 3) and has(n, 0):
                        a, z = g * GROUP, (g + 1) * GROUP
                        if j == 2:
                            make_hot(hot_block, block_c, BLOCKS, a, z)
                        else:
                            make_hot(hot_owner, owner_c, P, a, z).then_inc(hot_ready, 1)
                if has(n, LAG_PLACE):
                    cast_positions(place, slot, c - 1 if g < LAG_PLACE else c)

            dve.wait_ge(count_hot, CHUNKS * 2)
            copy_chunk(0, CHUNKS + 1)
            for n in range(GROUPS):
                step(0, n, n)
            with dve.Fori(1, CHUNKS) as c:
                dve.wait_ge(hot_ready, c * GROUPS)
                copy_chunk(c, c + (CHUNKS + 1))
                for g in range(GROUPS):
                    step(c, c * GROUPS + g, g)
            for n in range(CHUNKS * GROUPS, LAST_STEP + 1):
                step(CHUNKS, n, n % GROUPS)

            nc.vector.memset(x_sb[P - 32:P, :], 0.0).then_inc(x_cleared, 1)
            nc.vector.memset(run_sum[:, :, :], 0.0)
            nc.vector.memset(run_max[:, :, :], -FLT_MAX).then_inc(round_added, 1)
            dve.wait_ge(round_added, 1)
            dve.wait_ge(passes_ready, 1)
            passes = dve.value_load(passes_i[0:1, 0:1], min_val=1, max_val=-(-EDGES // WINDOW))
            ahead = SLOTS * ROUNDS
            with dve.Fori(0, passes) as q:
                with dve.Fori(0, ROUNDS) as r:
                    i = q * ROUNDS + r
                    nc.vector.tensor_copy(window_at[:, :], next_t[:, bass.ds(r * SLOTS, SLOTS)])
                    nc.vector.tensor_copy(left_s[:, :], left_t[:, bass.ds(r * SLOTS, SLOTS)])\
                        .then_inc(windows_placed, 1)
                    dve.wait_ge(windows_placed, i + 1)
                    for s in range(SLOTS):
                        w = window[:, s, :]
                        k = i * SLOTS + s
                        nc.vector.tensor_scalar(half[:, :], iota_f[:, :], left_s[:, s:s + 1], 0.5,
                                                ALU.is_lt, ALU.subtract).then_inc(masks_made, 1)
                        dve.wait_ge(masks_made, k * 2 + 1)
                        nc.vector.tensor_scalar(bound[:, :], half[:, :], FLT_MAX, 2.0, ALU.mult, ALU.mult)
                        nc.vector.tensor_scalar(keep[:, :], half[:, :], 0.5, -1.0, ALU.add, ALU.mult)\
                            .then_inc(masks_made, 1)
                        dve.wait_ge(masks_made, k * 2 + 2)
                        dve.wait_ge(window_loaded[s], i * 16 + 16)
                        nc.vector.tensor_tensor(clipped[:, :].rearrange("p (r f) -> p r f", f=FEAT),
                                                w.rearrange("p (r f) -> p r f", f=FEAT),
                                                bound[:, :].unsqueeze(2).to_broadcast([P, WINDOW, FEAT]), ALU.min)\
                            .then_inc(window_clipped, 1)
                        nc.vector.tensor_tensor(w.bitcast(I32).rearrange("p (r f) -> p r f", f=FEAT),
                                                w.bitcast(I32).rearrange("p (r f) -> p r f", f=FEAT),
                                                keep[:, :].unsqueeze(2).to_broadcast([P, WINDOW, FEAT]),
                                                ALU.bitwise_and).then_inc(window_masked, 1)
                        dve.wait_ge(window_clipped, k + 1)
                        nc.vector.tensor_reduce(part_max[:, s, :], clipped[:, :].rearrange("p (r f) -> p f r", f=FEAT),
                                                AXIS_X, ALU.max)
                        dve.wait_ge(window_masked, k + 1)
                        nc.vector.tensor_reduce(part_sum[:, s, :], w.rearrange("p (r f) -> p f r", f=FEAT),
                                                AXIS_X, ALU.add).then_inc(window_reduced, 1)
                        dve.wait_ge(window_reduced, k + 1)
                    mine = bass.ds(r * SLOTS, SLOTS)
                    nc.vector.tensor_tensor(run_max[:, mine, :], run_max[:, mine, :], part_max[:, :, :], ALU.max)
                    nc.vector.tensor_tensor(run_sum[:, mine, :], run_sum[:, mine, :], part_sum[:, :, :], ALU.add)\
                        .then_inc(round_added, 1)
                    dve.wait_ge(round_added, i + 2)
                nc.vector.tensor_scalar(next_t[:, :], next_t[:, :], float(WINDOW), float(EDGES), ALU.add, ALU.min)
                nc.vector.tensor_scalar(left_t[:, :], left_t[:, :], float(WINDOW), None, ALU.subtract)\
                    .then_inc(pass_moved, 1)
                dve.wait_ge(pass_moved, q + 1)

            dve.wait_ge(weights_loaded, 6 * 16)
            dve.wait_ge(x_loaded, 32)
            nc.vector.tensor_scalar(divisor[:, :], count_t[:, :], 1.0, None, ALU.max).then_inc(mlp_prep, 1)
            nc.vector.tensor_scalar(nonempty[:, :], count_t[:, :], 0.0, None, ALU.is_gt).then_inc(mlp_prep, 1)
            nc.vector.scalar_tensor_tensor(bias1[:, :], w1_u[:, :], u_sb[:, 0:1], b1_sb[:, :], ALU.mult, ALU.add)\
                .then_inc(mlp_prep, 1)
            nc.vector.tensor_tensor(x_sb[:, :].rearrange("p (b n) -> p b n", n=NODE_OUT),
                                    x_sb[:, :].rearrange("p (b n) -> p b n", n=NODE_OUT),
                                    b2_sb[:, :].unsqueeze(1).to_broadcast([P, BLOCKS, NODE_OUT]), ALU.add)\
                .then_inc(mlp_prep, 1)
            dve.wait_ge(mlp_prep, 4)
            nc.vector.reciprocal(divisor[:, :], divisor[:, :]).then_inc(mlp_prep, 1)
            dve.wait_ge(mlp_prep, 5)
            with dve.Fori(0, ROUNDS) as r:
                mine = bass.ds(r * SLOTS, SLOTS)
                nc.vector.tensor_copy(cat[:, :, 0:FEAT], run_sum[:, mine, :])
                nc.vector.tensor_tensor(cat[:, :, FEAT:2 * FEAT], run_max[:, mine, :],
                                        nonempty[:, mine].unsqueeze(2).to_broadcast([P, SLOTS, FEAT]), ALU.mult)
                nc.vector.tensor_tensor(cat[:, :, 2 * FEAT:CAT], run_sum[:, mine, :],
                                        divisor[:, mine].unsqueeze(2).to_broadcast([P, SLOTS, FEAT]), ALU.mult)\
                    .then_inc(cat_ready, 1)
                dve.wait_ge(out_summed, r + 1)
                cols = bass.ds(r * (SLOTS * NODE_OUT), SLOTS * NODE_OUT)
                nc.vector.tensor_tensor(x_sb[:, cols], x_sb[:, cols], misc_ps[:, 0:SLOTS * NODE_OUT], ALU.add)\
                    .then_inc(out_ready, 1)
                dve.wait_ge(out_ready, r + 1)


def kernel(x, src, dst, edge_attr_32, L0_gnn_u, L0_gnn_W1, L0_gnn_b1, L0_gnn_W2, L0_gnn_b2):
    import concourse.bacc as bacc
    from concourse.bass_utils import run_bass_kernel_spmd

    nc = bacc.Bacc("TRN2", target_bir_lowering=False, num_devices=1)
    given = {"x": x, "src": src, "edge_attr": edge_attr_32, "u": L0_gnn_u, "w1": L0_gnn_W1, "b1": L0_gnn_b1,
             "w2": L0_gnn_W2, "b2": L0_gnn_b2}
    arrays, aps = {}, {}
    for name, value in given.items():
        a = np.ascontiguousarray(value)
        arrays[f"in_{name}"] = a
        aps[name] = nc.dram_tensor(f"in_{name}", a.shape, mybir.dt.from_np(a.dtype), kind="ExternalInput").ap()
    edges, feat = aps["edge_attr"].shape
    out = nc.dram_tensor("out", aps["x"].shape, FP32, kind="ExternalOutput").ap()
    rows = nc.dram_tensor("sorted_rows", (edges + 64, feat), FP32, kind="Internal").ap()
    build(nc, aps["x"], aps["src"], aps["edge_attr"], aps["u"], aps["w1"], aps["b1"], aps["w2"], aps["b2"], out, rows)
    r = run_bass_kernel_spmd(nc, [arrays], core_ids=[0])
    return r.results[0]["out"]
```

```python
from contextlib import ExitStack

import numpy as np

import concourse.bass as bass
from concourse import mybir

FP32 = mybir.dt.float32
BF16 = mybir.dt.bfloat16
I32 = mybir.dt.int32
ALU = mybir.AluOpType
ACT = mybir.ActivationFunctionType
AXIS_X = mybir.AxisListType.X
FLT_MAX = float(np.finfo(np.float32).max)


def build(nc, x, src, edge_attr, u, w1, b1, w2, b2, out, rows):
    P = 128
    EDGES, FEAT = edge_attr.shape
    NODES, NODE_OUT = x.shape
    HID = w1.shape[1]
    BLOCKS = -(-NODES // P)
    TILES = EDGES // P
    GROUP = 5
    GROUPS = 5
    CHUNK = GROUP * GROUPS
    CHUNKS = TILES // CHUNK
    assert EDGES == P * CHUNK * CHUNKS
    WINDOW = 64
    SLOTS = 7
    HALVES = BLOCKS // SLOTS
    ROUNDS = HALVES // 2
    assert ROUNDS * 2 * SLOTS == BLOCKS
    FOLD = 8
    LAG_FOLD = 3
    CAT = 3 * FEAT
    FULL_P = NODES // BLOCKS
    REST = NODES - FULL_P * BLOCKS
    BANK_COLS = 512

    src_view = src.rearrange("(p t) -> p t", p=P)
    edge_view = edge_attr.rearrange("(p t) f -> p (t f)", p=P)

    ctx = ExitStack()
    with ctx:
        def sb(name, shape, dt):
            return ctx.enter_context(nc.sbuf_tensor(name, shape, dt))

        def ps(name, shape, dt):
            return ctx.enter_context(nc.psum_tensor(name, shape, dt))

        def sem(name):
            return ctx.enter_context(nc.semaphore(name))

        iota_i = sb("iota_i", [P, P], I32)
        iota_b = sb("iota_b", [P, P], BF16)
        iota_f = sb("iota_f", [P, WINDOW], FP32)
        before_f = sb("before_f", [P, P], FP32)
        before_b = sb("before_b", [P, P], BF16)
        ident_f = sb("ident_f", [P, P], FP32)
        ident_b = sb("ident_b", [P, P], BF16)
        zeros_b = sb("zeros_b", [P, P], BF16)
        zeros_f = sb("zeros_f", [P, P], FP32)
        late = sb("late", [P, (2 + HALVES) * SLOTS * NODE_OUT], FP32)
        src_i = late[:, GROUPS * GROUP * P:GROUPS * GROUP * P + TILES].bitcast(I32)
        hot_block_tf = late[0:BLOCKS, 0:GROUPS * GROUP * P].rearrange("p (g m) -> p g m", g=GROUPS)
        run_sum = sb("run_sum", [P, SLOTS + BLOCKS, FEAT], FP32)
        run_max = sb("run_max", [P, SLOTS + BLOCKS, FEAT], FP32)
        owner = run_sum[:, :, :].rearrange("p b f -> p (b f)")[:, 0:TILES]
        block_of = run_max[:, :, :].rearrange("p b f -> p (b f)")[:, 0:TILES]
        x_sb = sb("x_sb", [P, (2 + HALVES) * SLOTS * NODE_OUT], FP32)
        ids_2 = x_sb[:, :].bitcast(BF16)
        owner_2 = ids_2[:, 0:2 * TILES].rearrange("p (t w) -> p t w", w=2)
        block_2 = ids_2[:, BLOCKS * NODE_OUT:BLOCKS * NODE_OUT + 2 * TILES].rearrange("p (t w) -> p t w", w=2)
        hot_block = sb("hot_block", [P, CHUNK, BLOCKS], BF16)
        hot_owner = sb("hot_owner", [P, CHUNK, P], BF16)
        window = sb("window", [P, SLOTS, WINDOW * FEAT], FP32)
        lent = window[:, :, :].rearrange("p s n -> p (s n)").bitcast(BF16)
        hot_block_t = lent[0:BLOCKS, 0:CHUNK * P].rearrange("p (g m) -> p g m", g=GROUPS)
        earlier = lent[:, CHUNK * P:2 * CHUNK * P].rearrange("p (g m) -> p g m", g=GROUPS)
        start_sb = sb("start_sb", [BLOCKS, GROUP, P], FP32)
        picked = sb("picked", [P, GROUP, P], BF16)
        position_f = sb("position_f", [P, CHUNK], FP32)
        position = sb("position", [P, CHUNK], I32)
        edges = sb("edges", [P, GROUPS, GROUP * FEAT], FP32)
        count = sb("count", [BLOCKS, P], FP32)
        cumul = sb("cumul", [BLOCKS, P], FP32)
        block_base = sb("block_base", [BLOCKS, 1], FP32)
        offset = sb("offset", [BLOCKS, P], FP32)
        count_t = sb("count_t", [P, BLOCKS], FP32)
        left_t = sb("left_t", [P, BLOCKS + SLOTS], FP32)
        next_t = sb("next_t", [P, BLOCKS + SLOTS], FP32)
        most_p = sb("most_p", [P, 1], FP32)
        most = sb("most", [1, 1], FP32)
        passes_i = sb("passes_i", [1, 1], I32)
        masked = sb("masked", [P, 2, WINDOW * FEAT], FP32)
        iota_half = masked[:, 0, 0:BLOCKS]
        step_down = masked[0:BLOCKS, 1, 0:BLOCKS]
        window_at = sb("window_at", [P, 2, SLOTS], I32)
        left_s = sb("left_s", [P, SLOTS], FP32)
        valid = sb("valid", [P, 2, SLOTS, WINDOW], FP32)
        bound = sb("bound", [P, 2, SLOTS, WINDOW], FP32)
        part_sum = sb("part_sum", [P, 2, SLOTS, FEAT], FP32)
        part_max = sb("part_max", [P, 2, SLOTS, FEAT], FP32)
        divisor = sb("divisor", [P, BLOCKS], FP32)
        per_count = sb("per_count", [P, SLOTS + BLOCKS], FP32)
        nonempty = sb("nonempty", [P, SLOTS + BLOCKS], FP32)
        w1_sb = sb("w1_sb", [CAT, HID], FP32)
        w1_u = sb("w1_u", [HID, 1], FP32)
        b1_sb = sb("b1_sb", [HID, 1], FP32)
        u_sb = sb("u_sb", [HID, 1], FP32)
        bias1 = sb("bias1", [HID, 1], FP32)
        w2_sb = sb("w2_sb", [HID, NODE_OUT], FP32)
        b2_sb = sb("b2_sb", [P, NODE_OUT], FP32)
        cat = sb("cat", [P, SLOTS, CAT], FP32)
        cat_t = sb("cat_t", [CAT, SLOTS * P], FP32)
        hidden = sb("hidden", [HID, SLOTS * P], FP32)

        start_ps = ps("start_ps", [P, BANK_COLS], FP32)
        hot_t_ps = ps("hot_t_ps", [P, 2 * BANK_COLS], BF16)
        same_ps = ps("same_ps", [P, 2 * BANK_COLS], FP32)
        place_ps = ps("place_ps", [P, 3 * BANK_COLS], FP32)
        misc_ps = ps("misc_ps", [P, BANK_COLS], FP32)

        src_loaded = sem("src_loaded")
        weights_loaded = sem("weights_loaded")
        x_cleared = sem("x_cleared")
        x_loaded = sem("x_loaded")
        pad_written = sem("pad_written")
        const_made = sem("const_made")
        const_cast = sem("const_cast")
        split_done = sem("split_done")
        owner_paired = sem("owner_paired")
        results_cleared = sem("results_cleared")
        iota_moved = sem("iota_moved")
        step_made = sem("step_made")
        count_hot = sem("count_hot")
        count_signed = sem("count_signed")
        signs_copied = sem("signs_copied")
        counted = sem("counted")
        offset_step = sem("offset_step")
        offset_pe = sem("offset_pe")
        passes_ready = sem("passes_ready")
        hot_ready = sem("hot_ready")
        hot_transposed = sem("hot_transposed")
        hot_copied = sem("hot_copied")
        hot_cast = sem("hot_cast")
        same_ready = sem("same_ready")
        earlier_ready = sem("earlier_ready")
        start_copied = sem("start_copied")
        start_moved = sem("start_moved")
        place_ready = sem("place_ready")
        picked_sum = sem("picked_sum")
        position_ready = sem("position_ready")
        edges_loaded = [sem(f"edges_loaded{k}") for k in range(GROUPS)]
        edges_sent = [sem(f"edges_sent{k}") for k in range(GROUPS)]
        group_begun = sem("group_begun")
        windows_placed = sem("windows_placed")
        window_loaded = [sem(f"window_loaded{s}") for s in range(SLOTS)]
        left_copied = sem("left_copied")
        valid_made = sem("valid_made")
        sign_made = sem("sign_made")
        bound_made = sem("bound_made")
        window_clipped = sem("window_clipped")
        max_taken = sem("max_taken")
        window_masked = sem("window_masked")
        window_summed = sem("window_summed")
        sum_folded = sem("sum_folded")
        pass_moved = sem("pass_moved")
        pass_begun = sem("pass_begun")
        mlp_prep = sem("mlp_prep")
        x_biased = sem("x_biased")
        half_added = sem("half_added")
        room_added = sem("room_added")
        cat_ready = sem("cat_ready")
        cat_transposed = sem("cat_transposed")
        cat_copied = sem("cat_copied")
        hidden_summed = sem("hidden_summed")
        hidden_ready = sem("hidden_ready")
        out_summed = sem("out_summed")
        out_added = sem("out_added")
        out_ready = sem("out_ready")
        out_written = sem("out_written")

        PLACE_BANK = [0, 1, 0, 1, 2]
        PLACE_USER = [3, 3, 2, 2, 5]

        COUNT_SPANS = [(0, 7, 12), (12, 20, CHUNK)]
        sign_ps = same_ps[0:BLOCKS, 0:P]

        LAG_TRANSPOSE, LAG_SAME, LAG_EARLIER, LAG_PLACE = 1, 2, 3, 4
        LAST_STEP = CHUNKS * GROUPS - 1 + LAG_PLACE
        HALF = 2 * P
        BANK_TILES = BANK_COLS // P

        sum_banks = [place_ps[:, k * BANK_COLS:k * BANK_COLS + FOLD * FEAT] for k in range(2)]
        SPANS = [(0, 4), (4, SLOTS)]
        cat_banks = [same_ps[0:CAT, k * BANK_COLS:(k + 1) * BANK_COLS] for k in range(2)]
        hid_banks = [place_ps[:, 2 * BANK_COLS:3 * BANK_COLS], start_ps[:, :]]

        def load_passes(eng):
            eng.wait_ge(passes_ready, 1)
            return eng.value_load(passes_i[0:1, 0:1], min_val=1, max_val=-(-EDGES // WINDOW))

        def has(n, lag):
            return not isinstance(n, int) or lag <= n < CHUNKS * GROUPS + lag

        def place_slot(j):
            return place_ps[:, PLACE_BANK[j] * BANK_COLS:PLACE_BANK[j] * BANK_COLS + P]

        block = ctx.enter_context(nc.Block())

        @block.sync
        def _(sp):
            sp.dma_start(src_i, src_view).then_inc(src_loaded, 16)
            sp.wait_ge(const_made, 3)
            sp.dma_start(rows[EDGES:EDGES + WINDOW, :].rearrange("(p r) f -> p (r f)", p=16),
                         zeros_f[0:16, :]).then_inc(pad_written, 16)
            sp.dma_start(w1_sb[:, :], w1[0:CAT, :]).then_inc(weights_loaded, 16)
            sp.dma_start(w1_u[:, :], w1[CAT, :].rearrange("(h o) -> h o", o=1)).then_inc(weights_loaded, 16)
            sp.dma_start(b1_sb[:, :], b1.rearrange("(h o) -> h o", o=1)).then_inc(weights_loaded, 16)
            sp.dma_start(u_sb[:, :], u[0:1, :].to_broadcast([HID, 1])).then_inc(weights_loaded, 16)
            sp.dma_start(w2_sb[:, :], w2[:, :]).then_inc(weights_loaded, 16)
            sp.dma_start(b2_sb[:, :], b2.rearrange("(o n) -> o n", o=1).to_broadcast([P, NODE_OUT]))\
                .then_inc(weights_loaded, 16)

            def load_group(c, k):
                at = (c * CHUNK + k * GROUP) * FEAT
                sp.dma_start(edges[:, k, :], edge_view[:, bass.ds(at, GROUP * FEAT)]).then_inc(edges_loaded[k], 16)

            for k in range(GROUPS):
                load_group(0, k)
            with sp.Fori(1, CHUNKS) as c:
                for k in range(GROUPS):
                    sp.wait_ge(edges_sent[k], c * (16 * GROUP))
                    load_group(c, k)
            sp.wait_ge(x_cleared, 1)
            X0 = 2 * SLOTS * NODE_OUT
            sp.dma_start(x_sb[0:FULL_P, X0:], x[0:FULL_P * BLOCKS, :].rearrange("(p b) n -> p (b n)", b=BLOCKS))\
                .then_inc(x_loaded, 16)
            sp.dma_start(x_sb[FULL_P:FULL_P + 1, X0:X0 + REST * NODE_OUT],
                         x[FULL_P * BLOCKS:NODES, :].rearrange("(p b) n -> p (b n)", b=REST)).then_inc(x_loaded, 16)
            sp.wait_ge(pad_written, 16)
            sp.wait_ge(out_ready, 1)
            sp.dma_start(out[0:FULL_P * BLOCKS, :].rearrange("(p b) n -> p (b n)", b=BLOCKS), late[0:FULL_P, X0:])\
                .then_inc(out_written, 16)
            sp.dma_start(out[FULL_P * BLOCKS:NODES, :].rearrange("(p b) n -> p (b n)", b=REST),
                         late[FULL_P:FULL_P + 1, X0:X0 + REST * NODE_OUT]).then_inc(out_written, 16)
            sp.wait_ge(out_written, 32)

        @block.gpsimd
        def _(pool):
            nc.gpsimd.memset(before_f[:, :], 1.0).then_inc(const_made, 1)
            nc.gpsimd.memset(ident_f[:, :], 0.0).then_inc(const_made, 1)
            nc.gpsimd.memset(zeros_f[:, :], 0.0).then_inc(const_made, 1)
            nc.gpsimd.iota(iota_i[:, :], pattern=[[1, P]], base=0, channel_multiplier=0).then_inc(const_made, 1)
            pool.wait_ge(const_made, 4)
            nc.gpsimd.affine_select(out=before_f[:, :], in_=before_f[:, :], compare_op=ALU.is_gt, fill=0.0,
                                    base=0, pattern=[[1, P]], channel_multiplier=-1).then_inc(const_made, 1)
            nc.gpsimd.affine_select(out=ident_f[:, :], in_=ident_f[:, :], compare_op=ALU.not_equal, fill=1.0,
                                    base=0, pattern=[[1, P]], channel_multiplier=-1).then_inc(const_made, 1)

            nc.gpsimd.memset(step_down, 0.0).then_inc(step_made, 1)
            for k, (apart, factor) in enumerate(((0, 0.5), (1, -0.5), (1 - BLOCKS, 0.5))):
                pool.wait_ge(step_made, k + 1)
                nc.gpsimd.affine_select(out=step_down, in_=step_down, compare_op=ALU.not_equal, fill=factor,
                                        base=apart, pattern=[[1, BLOCKS]], channel_multiplier=-1)\
                    .then_inc(step_made, 1)

            pool.wait_ge(owner_paired, 1)
            pool.wait_ge(split_done, 5)
            nc.gpsimd.memset(run_sum[:, :, :], 0.0)
            pool.wait_ge(count_signed, CHUNKS * 2)
            nc.gpsimd.memset(run_max[:, :, :], -FLT_MAX).then_inc(results_cleared, 1)

            with pool.Fori(0, CHUNKS) as c:
                for k in range(GROUPS):
                    pool.wait_ge(position_ready, c * GROUPS + (k + 1))
                    pool.wait_ge(edges_loaded[k], c * 16 + 16)
                    pool.sem_inc(group_begun, 1)
                    for j in range(GROUP):
                        t = k * GROUP + j
                        nc.gpsimd.indirect_dma_start(
                            out=rows[:, :], out_offset=bass.IndirectOffsetOnAxis(ap=position[:, t:t + 1], axis=0),
                            in_=edges[:, k, j * FEAT:(j + 1) * FEAT], in_offset=None).then_inc(edges_sent[k], 16)
            for k in range(GROUPS):
                pool.wait_ge(edges_sent[k], CHUNKS * GROUP * 16)
            pool.wait_ge(pad_written, 16)
            passes = load_passes(pool)

            def gather(half, k):
                nc.gpsimd.indirect_dma_start(
                    out=window[:, k, :], out_offset=None, in_=rows[:, :],
                    in_offset=bass.IndirectOffsetOnAxis(ap=window_at[:, half, k:k + 1], axis=0))\
                    .then_inc(window_loaded[k], 16)

            pool.sem_inc(window_masked, 1)
            pool.wait_ge(windows_placed, 1)
            for s in range(SLOTS - 1):
                gather(0, s)
            with pool.Fori(0, passes * ROUNDS) as i:
                for h in range(2):
                    for s in range(SLOTS):
                        b = i * (2 * SLOTS) + (h * SLOTS + s)
                        k = (h * SLOTS + s) % 2
                        pool.wait_ge(window_summed, b + (LAG_FOLD - 1))
                        pool.wait_ge(window_clipped, b + 1)
                        nc.gpsimd.tensor_tensor(masked[:, k, :].rearrange("p (r f) -> p r f", f=FEAT),
                                                window[:, s, :].rearrange("p (r f) -> p r f", f=FEAT),
                                                valid[:, h, s, :].unsqueeze(2).to_broadcast([P, WINDOW, FEAT]),
                                                ALU.mult).then_inc(window_masked, 1)
                        pool.wait_ge(windows_placed, i * 2 + (h + (1 if s == 0 else 2)))
                        pool.wait_ge(window_masked, b + 1)
                        pool.wait_ge(max_taken, b + 1)
                        pool.sem_inc(group_begun, 1)
                        gather(h if s == 0 else 1 - h, (s - 1) % SLOTS)
            for s in range(SLOTS):
                pool.wait_ge(window_loaded[s], passes * (HALVES * 16) + (16 if s < SLOTS - 1 else 0))

        @block.tensor
        def _(pe):
            pe.wait_ge(const_cast, 4)
            nc.tensor.matmul(start_ps[0:BLOCKS, 0:P], zeros_b[:, 0:BLOCKS], zeros_b[:, :], start=True, stop=False)
            nc.tensor.matmul(sign_ps, zeros_b[:, 0:BLOCKS], zeros_b[:, :], start=True, stop=False)
            with pe.Fori(0, CHUNKS) as c:
                for k, (a, m, z) in enumerate(COUNT_SPANS):
                    pe.wait_ge(count_hot, c * 2 + (k + 1))
                    for t in range(a, m):
                        nc.tensor.matmul(start_ps[0:BLOCKS, 0:P], hot_block[:, t, :], hot_owner[:, t, :],
                                         start=False, stop=False)
                    pe.wait_ge(count_signed, c * 2 + (k + 1))
                    for t in range(m, z):
                        last = nc.tensor.matmul(sign_ps, hot_block[:, t, :], hot_owner[:, t, :],
                                                start=False, stop=False)
                    last.then_inc(counted, 1)
            nc.tensor.matmul(sign_ps, zeros_b[:, 0:BLOCKS], zeros_b[:, :], start=False, stop=True)\
                .then_inc(counted, 1)
            pe.wait_ge(step_made, 4)
            pe.wait_ge(signs_copied, 1)
            nc.tensor.matmul(start_ps[0:BLOCKS, 0:P], step_down, offset[:, :], start=False, stop=True)\
                .then_inc(counted, 1)

            pe.wait_ge(offset_step, 2)
            nc.tensor.matmul(misc_ps[0:BLOCKS, 0:1], before_f[0:BLOCKS, 0:BLOCKS], cumul[:, P - 1:P],
                             start=True, stop=True).then_inc(offset_pe, 1)
            pe.wait_ge(offset_step, 4)
            nc.tensor.matmul(start_ps[0:BLOCKS, 0:P], ident_f[0:BLOCKS, 0:BLOCKS], offset[:, :],
                             start=True, stop=False, skip_group_check=True).then_inc(start_moved, 1)
            nc.tensor.transpose(misc_ps[:, 128:128 + BLOCKS], offset[:, :], ident_f[0:BLOCKS, 0:BLOCKS])
            nc.tensor.transpose(misc_ps[:, 256:256 + BLOCKS], count[:, :], ident_f[0:BLOCKS, 0:BLOCKS])\
                .then_inc(offset_pe, 1)
            pe.wait_ge(offset_step, 7)
            nc.tensor.transpose(misc_ps[0:1, 0:P], most_p[:, :], ident_f[:, :]).then_inc(offset_pe, 1)

            def transpose_tile(m, slot, j):
                if j == 0:
                    pe.wait_ge(hot_ready, m + 1)
                    if not isinstance(m, int) or m > 0:
                        pe.wait_ge(hot_copied, m)
                last = nc.tensor.transpose(hot_t_ps[0:BLOCKS, j * P:(j + 1) * P],
                                           hot_block[:, slot * GROUP + j, :], ident_b[:, :])
                if j == GROUP - 1:
                    last.then_inc(hot_transposed, 1)

            def match_tile(m, slot, j):
                if j == 0:
                    pe.wait_ge(hot_cast, m + 1)
                if j in (0, BANK_TILES) and (not isinstance(m, int) or m > 0):
                    pe.wait_ge(earlier_ready, m * 2 - (1 if j == 0 else 0))
                hot = hot_block_t[:, slot, j * P:(j + 1) * P]
                last = nc.tensor.matmul(same_ps[:, j * P:(j + 1) * P], hot, hot, start=True, stop=True)
                if j in (BANK_TILES - 1, GROUP - 1):
                    last.then_inc(same_ready, 1)

            def place_tile(m, slot, j):
                t = slot * GROUP + j
                if j == 0:
                    pe.wait_ge(earlier_ready, m * 2 + 2)
                pe.wait_ge(start_copied, m * GROUP + (j + 1))
                nc.tensor.matmul(start_ps[0:BLOCKS, 0:P], hot_block[:, t, :], hot_owner[:, t, :],
                                 start=False, stop=False, skip_group_check=True).then_inc(start_moved, 1)
                if not isinstance(m, int) or m * GROUP + j >= PLACE_USER[j]:
                    pe.wait_ge(picked_sum, m * GROUP + (j + 1 - PLACE_USER[j]))
                nc.tensor.matmul(place_slot(j), hot_block_tf[:, slot, j * P:(j + 1) * P], start_sb[:, j, :],
                                 start=True, stop=False)
                nc.tensor.matmul(place_slot(j), earlier[:, slot, j * P:(j + 1) * P], hot_owner[:, t, :],
                                 start=False, stop=True).then_inc(place_ready, 1)

            def step(n, g):
                fill = []
                if has(n, LAG_TRANSPOSE):
                    fill += [(transpose_tile, LAG_TRANSPOSE, j) for j in range(GROUP)]
                if has(n, LAG_SAME):
                    fill += [(match_tile, LAG_SAME, j) for j in range(GROUP)]
                for j in range(GROUP):
                    if has(n, LAG_PLACE):
                        place_tile(n - LAG_PLACE, (g - LAG_PLACE) % GROUPS, j)
                    for work, lag, k in fill[2 * j:2 * j + 2]:
                        work(n - lag, (g - lag) % GROUPS, k)

            for n in range(GROUPS):
                step(n, n)
            with pe.Fori(1, CHUNKS) as c:
                for g in range(GROUPS):
                    step(c * GROUPS + g, g)
            for n in range(CHUNKS * GROUPS, LAST_STEP + 1):
                step(n, n % GROUPS)

            passes = load_passes(pe)
            pe.wait_ge(mlp_prep, 4)
            for b in range(LAG_FOLD):
                if b == 2:
                    pe.wait_ge(sum_folded, 1)
                nc.tensor.matmul(sum_banks[(b + 1) % 2], zeros_b[:, :], hot_owner[:, 0:2, :], start=True, stop=True)\
                    .then_inc(window_summed, 1)
            nc.tensor.matmul(misc_ps[:, 0:SLOTS * NODE_OUT], zeros_b[:, :],
                             hot_owner[:, 0:4, 0:SLOTS * NODE_OUT // 4], start=True, stop=True)\
                .then_inc(out_summed, 1)

            def sum_window(b, k):
                pe.wait_ge(window_masked, b + 2)
                pe.wait_ge(sum_folded, b + (LAG_FOLD - 1))
                cols = FOLD * FEAT
                for r in range(WINDOW // FOLD):
                    last = nc.tensor.matmul(sum_banks[k], ident_f[:, :], masked[:, k, r * cols:(r + 1) * cols],
                                            start=(r == 0), stop=(r == WINDOW // FOLD - 1))
                last.then_inc(window_summed, 1)

            def transpose_cat(f):
                pe.wait_ge(cat_ready, f + 1)
                for n, (a, z) in enumerate(SPANS):
                    for s in range(a, z):
                        last = nc.tensor.transpose(cat_banks[n][:, (s - a) * P:(s - a + 1) * P], cat[:, s, :],
                                                   ident_f[:, :])
                    last.then_inc(cat_transposed, 1)

            def sum_hidden(f):
                for n, (a, z) in enumerate(SPANS):
                    pe.wait_ge(cat_copied, f * 2 + (n + 1))
                    nc.tensor.matmul(hid_banks[n][:, 0:(z - a) * P], w1_sb[:, :], cat_t[:, a * P:z * P],
                                     start=True, stop=True).then_inc(hidden_summed, 1)

            def sum_out(f):
                pe.wait_ge(out_added, f + 1)
                for n, (a, z) in enumerate(SPANS):
                    pe.wait_ge(hidden_ready, f * 2 + (n + 1))
                    for s in range(a, z):
                        last = nc.tensor.matmul(misc_ps[:, s * NODE_OUT:(s + 1) * NODE_OUT],
                                                hidden[:, s * P:(s + 1) * P], w2_sb[:, :], start=True, stop=True)
                last.then_inc(out_summed, 1)

            with pe.Fori(0, passes * ROUNDS) as i:
                for h in range(2):
                    for s in range(SLOTS):
                        sum_window(i * (2 * SLOTS) + (h * SLOTS + s), (h * SLOTS + s) % 2)
                        for at, work in ((2, transpose_cat), (3, sum_hidden), (4, sum_out)):
                            if s == at:
                                work(i * 2 + h)
            for work in (transpose_cat, sum_hidden, sum_out):
                work(passes * HALVES)

        @block.scalar
        def _(act):
            act.wait_ge(split_done, 3)
            nc.scalar.activation(owner_2, owner.unsqueeze(2).to_broadcast([P, TILES, 2]), ACT.Copy)\
                .then_inc(owner_paired, 1)

            act.wait_ge(split_done, 4)
            act.wait_ge(iota_moved, 1)

            def sign_chunk(c):
                for k, (a, m, z) in enumerate(COUNT_SPANS):
                    if not isinstance(c, int):
                        act.wait_ge(counted, c * 2 + (k - 1))
                    for t in range(m, z):
                        last = nc.scalar.activation(hot_block[:, t, :], iota_half, ACT.Sign, scale=-1.0,
                                                    bias=block_of[:, bass.ds(c * CHUNK + t, 1)])
                    last.then_inc(count_signed, 1)

            sign_chunk(0)
            with act.Fori(1, CHUNKS) as c:
                sign_chunk(c)

            def copy_start(m, j):
                act.wait_ge(start_moved, m * GROUP + (j + 1))
                if not isinstance(m, int) or m > 0:
                    act.wait_ge(place_ready, m * GROUP + (j + 1 - GROUP))
                nc.scalar.activation(start_sb[:, j, :], start_ps[0:BLOCKS, 0:P], ACT.Copy).then_inc(start_copied, 1)

            def step(n, g):
                slot = (g - LAG_TRANSPOSE) % GROUPS
                for j in range(GROUP):
                    if has(n, LAG_PLACE):
                        copy_start(n - LAG_PLACE, j)
                    if j == 3 and has(n, LAG_TRANSPOSE):
                        act.wait_ge(hot_transposed, n - LAG_TRANSPOSE + 1)
                        nc.scalar.activation(hot_block_tf[:, slot, 0:HALF], hot_t_ps[0:BLOCKS, 0:HALF], ACT.Copy)
                if has(n, LAG_TRANSPOSE):
                    nc.scalar.activation(hot_block_tf[:, slot, HALF:], hot_t_ps[0:BLOCKS, HALF:GROUP * P], ACT.Copy)\
                        .then_inc(hot_copied, 1)

            for n in range(GROUPS):
                step(n, n)
            with act.Fori(1, CHUNKS) as c:
                for g in range(GROUPS):
                    step(c * GROUPS + g, g)
            for n in range(CHUNKS * GROUPS, LAST_STEP + 1):
                step(n, n % GROUPS)

            passes = load_passes(act)
            act.wait_ge(mlp_prep, 4)
            def concatenate(f, col):
                act.wait_ge(half_added, f + 1)
                nc.scalar.activation(cat[:, :, 0:FEAT], run_sum[:, bass.ds(col, SLOTS), :], ACT.Copy)
                for s in range(SLOTS):
                    at = bass.ds(col + s, 1)
                    nc.scalar.activation(cat[:, s, FEAT:2 * FEAT], run_max[:, at, :], ACT.Copy, scale=nonempty[:, at])
                    last = nc.scalar.activation(cat[:, s, 2 * FEAT:CAT], run_sum[:, at, :], ACT.Copy,
                                                scale=per_count[:, at])
                last.then_inc(cat_ready, 1)

            def make_bounds(f, half):
                act.wait_ge(valid_made, f + 1)
                nc.scalar.activation(bound[:, half, :, :], valid[:, half, :, :], ACT.Copy, scale=2.0, bias=-1.0)\
                    .then_inc(sign_made, 1)
                act.wait_ge(sign_made, f + 1)
                nc.scalar.activation(bound[:, half, :, :], bound[:, half, :, :], ACT.Copy, scale=FLT_MAX)\
                    .then_inc(bound_made, 1)

            def mlp_half(f):
                for n, (a, z) in enumerate(SPANS):
                    act.wait_ge(cat_transposed, f * 2 + (n + 1))
                    nc.scalar.activation(cat_t[:, a * P:z * P], cat_banks[n][:, 0:(z - a) * P], ACT.Copy)\
                        .then_inc(cat_copied, 1)
                for n, (a, z) in enumerate(SPANS):
                    act.wait_ge(hidden_summed, f * 2 + (n + 1))
                    nc.scalar.activation(hidden[:, a * P:z * P], hid_banks[n][:, 0:(z - a) * P],
                                         ACT.Relu, bias=bias1[:, 0:1]).then_inc(hidden_ready, 1)

            make_bounds(0, 0)
            with act.Fori(0, passes) as q:
                with act.Fori(0, ROUNDS) as r:
                    for h in range(2):
                        f = q * HALVES + (r * 2 + h)
                        concatenate(f, r * (2 * SLOTS) + h * SLOTS)
                        make_bounds(f + 1, 1 - h)
                        mlp_half(f)
            concatenate(passes * HALVES, BLOCKS)
            mlp_half(passes * HALVES)

        @block.vector
        def _(dve):
            nc.vector.memset(zeros_b[:, :], 0.0).then_inc(const_cast, 1)
            dve.wait_ge(const_made, 6)
            nc.vector.tensor_copy(iota_b[:, :], iota_i[:, :])
            nc.vector.tensor_copy(iota_f[:, :], iota_i[:, 0:WINDOW]).then_inc(const_cast, 1)
            nc.vector.tensor_copy(before_b[:, :], before_f[:, :]).then_inc(const_cast, 1)
            nc.vector.tensor_copy(ident_b[:, :], ident_f[:, :]).then_inc(const_cast, 1)
            dve.wait_ge(src_loaded, 16)
            nc.vector.tensor_copy(block_of, src_i).then_inc(split_done, 1)
            dve.wait_ge(split_done, 1)
            nc.vector.tensor_scalar(src_i, block_of, -(BLOCKS - 1) / 2, 1.0 / BLOCKS, ALU.add, ALU.mult)\
                .then_inc(split_done, 1)
            dve.wait_ge(split_done, 2)
            nc.vector.tensor_copy(owner, src_i).then_inc(split_done, 1)
            dve.wait_ge(split_done, 3)
            nc.vector.scalar_tensor_tensor(block_of, owner, -float(BLOCKS), block_of,
                                           ALU.mult, ALU.add).then_inc(split_done, 1)
            dve.wait_ge(split_done, 4)
            nc.vector.tensor_copy(block_2, block_of.unsqueeze(2).to_broadcast([P, TILES, 2]))\
                .then_inc(split_done, 1)
            dve.wait_ge(const_cast, 4)
            nc.vector.tensor_scalar(iota_half, iota_b[:, 0:BLOCKS], -0.5, None, ALU.add).then_inc(iota_moved, 1)
            dve.wait_ge(split_done, 5)
            dve.wait_ge(owner_paired, 1)

            def make_hot(hot, ids, values, c, a, z):
                pairs = values // 2
                return nc.vector.tensor_tensor(
                    hot[:, a:z, :].rearrange("p t (v w) -> p t v w", w=2),
                    ids[:, bass.ds(c * CHUNK + a, z - a), :].unsqueeze(2).to_broadcast([P, z - a, pairs, 2]),
                    iota_b[:, 0:values].rearrange("p (v w) -> p v w", w=2).unsqueeze(1)
                    .to_broadcast([P, z - a, pairs, 2]), ALU.is_equal)

            def count_chunk(c):
                for k, (a, m, z) in enumerate(COUNT_SPANS):
                    if not isinstance(c, int):
                        dve.wait_ge(counted, c * 2 + (k - 1))
                    make_hot(hot_block, block_2, BLOCKS, c, a, m)
                    make_hot(hot_owner, owner_2, P, c, a, z).then_inc(count_hot, 1)

            count_chunk(0)
            with dve.Fori(1, CHUNKS) as c:
                count_chunk(c)

            dve.wait_ge(counted, CHUNKS * 2 + 1)
            nc.vector.tensor_copy(offset[:, :], sign_ps).then_inc(signs_copied, 1)
            dve.wait_ge(counted, CHUNKS * 2 + 2)
            nc.vector.tensor_copy(count[:, :], start_ps[0:BLOCKS, 0:P]).then_inc(offset_step, 1)
            dve.wait_ge(offset_step, 1)
            nc.vector.tensor_tensor_scan(cumul[:, :], count[:, :], zeros_f[0:BLOCKS, :], 0.0, ALU.add, ALU.add)\
                .then_inc(offset_step, 1)
            dve.wait_ge(offset_pe, 1)
            dve.wait_ge(offset_step, 2)
            nc.vector.tensor_copy(block_base[:, :], misc_ps[0:BLOCKS, 0:1]).then_inc(offset_step, 1)
            dve.wait_ge(offset_step, 3)
            nc.vector.scalar_tensor_tensor(offset[:, :], cumul[:, :], block_base[:, 0:1], count[:, :],
                                           ALU.add, ALU.subtract).then_inc(offset_step, 1)
            dve.wait_ge(offset_pe, 2)
            nc.vector.tensor_copy(next_t[:, 0:BLOCKS], misc_ps[:, 128:128 + BLOCKS]).then_inc(offset_step, 1)
            nc.vector.tensor_copy(count_t[:, :], misc_ps[:, 256:256 + BLOCKS]).then_inc(offset_step, 1)
            dve.wait_ge(offset_step, 6)
            nc.vector.reduce_max(most_p[:, :], count_t[:, :], axis=AXIS_X).then_inc(offset_step, 1)
            nc.vector.tensor_copy(left_t[:, 0:BLOCKS], count_t[:, :]).then_inc(offset_step, 1)
            dve.wait_ge(offset_pe, 3)
            nc.vector.reduce_max(most[:, :], misc_ps[0:1, 0:P], axis=AXIS_X).then_inc(offset_step, 1)
            dve.wait_ge(offset_step, 9)
            nc.vector.tensor_scalar(passes_i[:, :], most[:, :], (WINDOW - 1) / 2, 1.0 / WINDOW, ALU.add, ALU.mult)\
                .then_inc(passes_ready, 1)

            def cast_hot(m, slot):
                dve.wait_ge(hot_copied, m + 1)
                nc.vector.tensor_copy(hot_block_t[:, slot, :], hot_block_tf[:, slot, :]).then_inc(hot_cast, 1)

            def mark_earlier(m, slot, part):
                a, z = ((0, BANK_TILES), (BANK_TILES, GROUP))[part]
                dve.wait_ge(same_ready, m * 2 + (part + 1))
                nc.vector.tensor_tensor(earlier[:, slot, a * P:z * P].rearrange("p (j m) -> p j m", j=z - a),
                                        same_ps[:, a * P:z * P].rearrange("p (j m) -> p j m", j=z - a),
                                        before_b[:, :].unsqueeze(1).to_broadcast([P, z - a, P]), ALU.mult)\
                    .then_inc(earlier_ready, 1)

            def pick_position(m, slot, j):
                t = slot * GROUP + j
                dve.wait_ge(place_ready, m * GROUP + (j + 1))
                nc.vector.tensor_tensor_reduce(out=picked[:, j, :], in0=place_slot(j), in1=hot_owner[:, t, :],
                                               scale=1.0, scalar=0.0, op0=ALU.mult, op1=ALU.add,
                                               accum_out=position_f[:, t:t + 1]).then_inc(picked_sum, 1)

            def cast_positions(m, slot, sent):
                dve.wait_ge(picked_sum, m * GROUP + GROUP)
                if not isinstance(m, int) or m >= GROUPS:
                    dve.wait_ge(edges_sent[slot], sent * (16 * GROUP))
                mine = slice(slot * GROUP, (slot + 1) * GROUP)
                nc.vector.tensor_copy(position[:, mine], position_f[:, mine]).then_inc(position_ready, 1)

            def step(c, n, g):
                if has(n, LAG_SAME):
                    cast_hot(n - LAG_SAME, (g - LAG_SAME) % GROUPS)
                place, slot = n - LAG_PLACE, (g - LAG_PLACE) % GROUPS
                for j in range(GROUP):
                    if has(n, LAG_PLACE):
                        pick_position(place, slot, j)
                    if j in (0, 1) and has(n, LAG_EARLIER):
                        mark_earlier(n - LAG_EARLIER, (g - LAG_EARLIER) % GROUPS, j)
                    if j in (2, 3) and has(n, 0):
                        a, z = g * GROUP, (g + 1) * GROUP
                        if j == 2:
                            make_hot(hot_block, block_2, BLOCKS, c, a, z)
                        else:
                            make_hot(hot_owner, owner_2, P, c, a, z).then_inc(hot_ready, 1)
                if has(n, LAG_PLACE):
                    cast_positions(place, slot, c - 1 if g < LAG_PLACE else c)

            for n in range(GROUPS):
                step(0, n, n)
            with dve.Fori(1, CHUNKS) as c:
                for g in range(GROUPS):
                    step(c, c * GROUPS + g, g)
            for n in range(CHUNKS * GROUPS, LAST_STEP + 1):
                step(CHUNKS, n, n % GROUPS)

            nc.vector.memset(x_sb[P - 32:P, 2 * SLOTS * NODE_OUT:], 0.0)
            nc.vector.memset(x_sb[:, 0:2 * SLOTS * NODE_OUT], 0.0).then_inc(x_cleared, 1)
            nc.vector.memset(part_max[:, :, :, :], -FLT_MAX).then_inc(max_taken, 1)
            nc.vector.memset(part_sum[:, :, :, :], 0.0)
            nc.vector.memset(cat[:, :, :], 0.0)
            dve.wait_ge(weights_loaded, 6 * 16)
            nc.vector.tensor_scalar(divisor[:, :], count_t[:, :], 1.0, None, ALU.max).then_inc(mlp_prep, 1)
            nc.vector.tensor_scalar(nonempty[:, SLOTS:], count_t[:, :], 0.0, None, ALU.is_gt).then_inc(mlp_prep, 1)
            nc.vector.memset(nonempty[:, 0:SLOTS], 0.0)
            nc.vector.memset(per_count[:, 0:SLOTS], 0.0)
            nc.vector.scalar_tensor_tensor(bias1[:, :], w1_u[:, :], u_sb[:, 0:1], b1_sb[:, :], ALU.mult, ALU.add)\
                .then_inc(mlp_prep, 1)
            dve.wait_ge(mlp_prep, 3)
            nc.vector.reciprocal(per_count[:, SLOTS:], divisor[:, :]).then_inc(mlp_prep, 1)
            dve.wait_ge(mlp_prep, 4)
            dve.wait_ge(max_taken, 1)
            dve.wait_ge(results_cleared, 1)
            passes = load_passes(dve)

            def place_windows(col, half):
                nc.vector.tensor_copy(window_at[:, half, :], next_t[:, bass.ds(col, SLOTS)]).then_inc(windows_placed, 1)

            def make_masks(f, col, half):
                nc.vector.tensor_copy(left_s[:, :], left_t[:, bass.ds(col, SLOTS)]).then_inc(left_copied, 1)
                dve.wait_ge(left_copied, f + 1)
                nc.vector.tensor_tensor(valid[:, half, :, :],
                                        iota_f[:, :].unsqueeze(1).to_broadcast([P, SLOTS, WINDOW]),
                                        left_s[:, :].unsqueeze(2).to_broadcast([P, SLOTS, WINDOW]), ALU.is_lt)\
                    .then_inc(valid_made, 1)

            def rows_of(s):
                return window[:, s, :].rearrange("p (r f) -> p r f", f=FEAT)

            def clip_window(f, half, s):
                w = rows_of(s)
                if s == 0:
                    dve.wait_ge(bound_made, f + 1)
                dve.wait_ge(window_loaded[s], f * 16 + 16)
                nc.vector.tensor_tensor(w, w, bound[:, half, s, :].unsqueeze(2).to_broadcast([P, WINDOW, FEAT]), ALU.min)\
                    .then_inc(window_clipped, 1)

            def take_max(b, half, s):
                dve.wait_ge(window_clipped, b + 1)
                nc.vector.tensor_reduce(part_max[:, half, s, :], rows_of(s).rearrange("p r f -> p f r"), AXIS_X,
                                        ALU.max)\
                    .then_inc(max_taken, 1)

            def fold_sum(count, half, s):
                dve.wait_ge(window_summed, count)
                nc.vector.tensor_reduce(part_sum[:, half, s, :],
                                        sum_banks[(half * SLOTS + s) % 2].rearrange("p (r f) -> p f r", f=FEAT),
                                        AXIS_X, ALU.add).then_inc(sum_folded, 1)

            def add_half(f, col, half, taken, folded):
                mine = bass.ds(col, SLOTS)
                dve.wait_ge(max_taken, taken)
                dve.wait_ge(sum_folded, folded)
                nc.vector.tensor_tensor(run_max[:, mine, :], run_max[:, mine, :], part_max[:, half, :, :], ALU.max)
                nc.vector.tensor_tensor(run_sum[:, mine, :], run_sum[:, mine, :], part_sum[:, half, :, :], ALU.add)\
                    .then_inc(half_added, 1)

            def add_out(f, col):
                dve.wait_ge(out_summed, f + 1)
                cols = bass.ds(col * NODE_OUT, SLOTS * NODE_OUT)
                nc.vector.tensor_tensor(late[:, cols], x_sb[:, cols], misc_ps[:, 0:SLOTS * NODE_OUT], ALU.add)\
                    .then_inc(out_added, 1)

            dve.wait_ge(x_loaded, 32)
            nc.vector.tensor_tensor(x_sb[:, :].rearrange("p (b n) -> p b n", n=NODE_OUT),
                                    x_sb[:, :].rearrange("p (b n) -> p b n", n=NODE_OUT),
                                    b2_sb[:, :].unsqueeze(1).to_broadcast([P, (2 + HALVES) * SLOTS, NODE_OUT]),
                                    ALU.add).then_inc(x_biased, 1)
            dve.wait_ge(x_biased, 1)
            place_windows(0, 0)
            make_masks(0, 0, 0)
            with dve.Fori(0, passes) as q:
                nc.vector.tensor_scalar(left_t[:, BLOCKS:], left_t[:, 0:SLOTS], float(WINDOW), None, ALU.subtract)
                nc.vector.tensor_scalar(next_t[:, BLOCKS:], next_t[:, 0:SLOTS], float(WINDOW), float(EDGES),
                                        ALU.add, ALU.min).then_inc(pass_moved, 1)
                dve.wait_ge(pass_moved, q * 2 + 1)
                dve.sem_inc(pass_begun, 1)
                with dve.Fori(0, ROUNDS) as r:
                    for h in range(2):
                        f = q * HALVES + (r * 2 + h)
                        col = r * (2 * SLOTS) + h * SLOTS
                        place_windows(col + SLOTS, 1 - h)
                        for s in range(SLOTS):
                            b = q * BLOCKS + (r * (2 * SLOTS) + (h * SLOTS + s))
                            clip_window(f, h, s)
                            if s == LAG_FOLD:
                                add_half(f, col, 1 - h, b + (1 - LAG_FOLD), b)
                            back = s - LAG_FOLD
                            fold_sum(b + 1, h if back >= 0 else 1 - h, back % SLOTS)
                            take_max(b, h, s)
                            if s == LAG_FOLD:
                                make_masks(f + 1, col + SLOTS, 1 - h)
                            if s == 1:
                                add_out(f, col)
                dve.wait_ge(windows_placed, q * HALVES + (HALVES + 1))
                nc.vector.tensor_scalar(next_t[:, 0:BLOCKS], next_t[:, 0:BLOCKS], float(WINDOW), float(EDGES),
                                        ALU.add, ALU.min)
                nc.vector.tensor_scalar(left_t[:, 0:BLOCKS], left_t[:, 0:BLOCKS], float(WINDOW), None, ALU.subtract)\
                    .then_inc(pass_moved, 1)
                dve.wait_ge(pass_moved, q * 2 + 2)
                dve.sem_inc(pass_begun, 1)

            halves, blocks = passes * HALVES, passes * BLOCKS
            for k in range(LAG_FOLD):
                fold_sum(blocks + (k + 1), 1, SLOTS - LAG_FOLD + k)
            last, room = slice(BLOCKS, BLOCKS + SLOTS), slice(0, SLOTS)
            nc.vector.tensor_tensor(run_max[:, last, :], run_max[:, last, :], run_max[:, room, :], ALU.max)
            nc.vector.tensor_tensor(run_sum[:, last, :], run_sum[:, last, :], run_sum[:, room, :], ALU.add)\
                .then_inc(room_added, 1)
            dve.wait_ge(room_added, 1)
            add_half(halves, BLOCKS, 1, blocks + 1, blocks + LAG_FOLD)
            add_out(halves, BLOCKS)
            add_out(halves + 1, BLOCKS + SLOTS)
            dve.wait_ge(out_added, halves + 2)
            nc.vector.sem_inc(out_ready, 1)


def kernel(x, src, dst, edge_attr_32, L0_gnn_u, L0_gnn_W1, L0_gnn_b1, L0_gnn_W2, L0_gnn_b2):
    import concourse.bacc as bacc
    from concourse.bass_utils import run_bass_kernel_spmd

    nc = bacc.Bacc("TRN2", target_bir_lowering=False, num_devices=1)
    given = {"x": x, "src": src, "edge_attr": edge_attr_32, "u": L0_gnn_u, "w1": L0_gnn_W1, "b1": L0_gnn_b1,
             "w2": L0_gnn_W2, "b2": L0_gnn_b2}
    arrays, aps = {}, {}
    for name, value in given.items():
        a = np.ascontiguousarray(value)
        arrays[f"in_{name}"] = a
        aps[name] = nc.dram_tensor(f"in_{name}", a.shape, mybir.dt.from_np(a.dtype), kind="ExternalInput").ap()
    edges, feat = aps["edge_attr"].shape
    out = nc.dram_tensor("out", aps["x"].shape, FP32, kind="ExternalOutput").ap()
    rows = nc.dram_tensor("sorted_rows", (edges + 64, feat), FP32, kind="Internal").ap()
    build(nc, aps["x"], aps["src"], aps["edge_attr"], aps["u"], aps["w1"], aps["b1"], aps["w2"], aps["b2"], out, rows)
    r = run_bass_kernel_spmd(nc, [arrays], core_ids=[0])
    return r.results[0]["out"]
```
